# Optimizing a Trainium2 kernel written in Bass

```python
import numpy as np
import jax
import jax.numpy as jnp

def _softmax(x, axis=-1):
    return jax.nn.softmax(x, axis=axis)

def _gelu(x):
    return jax.nn.gelu(x, approximate=True)

def _silu(x):
    return jax.nn.silu(x)

def _sigmoid(x):
    return jax.nn.sigmoid(x)

def _layernorm(x, axis=-1, eps=1e-05):
    m = jnp.mean(x, axis=axis, keepdims=True)
    v = jnp.var(x, axis=axis, keepdims=True)
    return (x - m) / jnp.sqrt(v + eps)

def _scatter_add(tgt, idx, src, axis=0):
    return tgt.at[idx].add(src)

def _segment_sum(src, seg, n):
    return jax.ops.segment_sum(src, seg, n)
kernel_name = 'mk_xattn_ffn_d2_seqx_r2_28844b'

def setup_inputs(seed: int=0):
    np.random.seed(seed)
    _w = jnp.asarray

    def _rec_inputs():
        import jax
        import jax.numpy as jnp
        _rk = jax.random.key(seed)
        x = -0.0002928 + 1 * jax.random.normal(jax.random.fold_in(_rk, 1), (16, 256, 512), jnp.float32)
        _lenS = 256 - jax.random.randint(jax.random.fold_in(_rk, 7), (16,), 0, max(1, 256 // 4) + 1, jnp.int32)
        _lenS2 = 256 - jax.random.randint(jax.random.fold_in(_rk, 8), (16,), 0, max(1, 256 // 4) + 1, jnp.int32)
        _ctx_768P = jax.random.normal(jax.random.fold_in(_rk, 11), (16, 16, 384), jnp.float32)
        _ctx_768c = jax.random.dirichlet(jax.random.fold_in(_rk, 511), 0.3 * jnp.ones((16,), jnp.float32), (16, 256))
        _ctx_768t = jnp.einsum('bsk,bkd->bsd', _ctx_768c, _ctx_768P)
        _ctx_768t = _ctx_768t * jax.lax.rsqrt(jnp.mean(jnp.square(_ctx_768t)) + 1e-12) * 0.953939
        ctx_768 = 2.09791e-05 + 1.00001 * (_ctx_768t + 0.3 * jax.random.normal(jax.random.fold_in(_rk, 611), (16, 256, 384), jnp.float32))
        return (x, ctx_768)
    x, ctx_768 = _rec_inputs()

    def _L0_xattn_setup():
        import jax, jax.numpy as jnp
        import numpy as np
        QUERY_DIM, KV_DIM, EMBED_DIM, NUM_HEADS = (512, 384, 512, 16)
        HEAD_DIM = EMBED_DIM // NUM_HEADS
        SCALE = HEAD_DIM ** (-0.5)
        LN_EPS = 1e-05

        def _l2norm(x, eps=1e-12):
            n = jnp.sqrt(jnp.sum(x * x, axis=-1, keepdims=True))
            return x / jnp.maximum(n, eps)
        key = jax.random.key(seed)
        ks = jax.random.split(key, 12)
        B, Nq, Nk = (2, 1024, 1024)
        s = lambda d: 1.0 / np.sqrt(d)
        return {'query': jax.random.normal(ks[0], (B, Nq, QUERY_DIM), jnp.float32), 'key': jax.random.normal(ks[1], (B, Nk, KV_DIM), jnp.float32), 'value': jax.random.normal(ks[2], (B, Nk, KV_DIM), jnp.float32), 'Wq': jax.random.normal(ks[3], (QUERY_DIM, EMBED_DIM), jnp.float32) * s(QUERY_DIM), 'bq': jnp.zeros((EMBED_DIM,), jnp.float32), 'Wk': jax.random.normal(ks[4], (KV_DIM, EMBED_DIM), jnp.float32) * s(KV_DIM), 'bk': jnp.zeros((EMBED_DIM,), jnp.float32), 'Wv': jax.random.normal(ks[5], (KV_DIM, EMBED_DIM), jnp.float32) * s(KV_DIM), 'bv': jnp.zeros((EMBED_DIM,), jnp.float32), 'Wo': jax.random.normal(ks[6], (EMBED_DIM, EMBED_DIM), jnp.float32) * s(EMBED_DIM), 'bo': jnp.zeros((EMBED_DIM,), jnp.float32), 'ln_gamma': jnp.ones((EMBED_DIM,), jnp.float32), 'ln_beta': jnp.zeros((EMBED_DIM,), jnp.float32)}
    _L0_xattn_all = _L0_xattn_setup()
    _L0_xattn_in = {k: v for k, v in _L0_xattn_all.items() if k in ('Wq', 'bq', 'Wk', 'bk', 'Wv', 'bv', 'Wo', 'bo', 'ln_gamma', 'ln_beta')}
    del _L0_xattn_all

    def _L0_ffn_setup():
        import jax, jax.numpy as jnp
        import numpy as np
        IN_FEATURES = 512
        ACT_BITS = 4

        def _hadamard(size: int) -> np.ndarray:
            h = np.array([[1.0]], dtype=np.float64)
            while h.shape[0] < size:
                h = np.block([[h, h], [h, -h]])
            return (h / np.sqrt(size)).astype(np.float32)

        def _quantize_activations(x, bits=ACT_BITS):
            pos = 2 ** (bits - 1) - 1
            neg = 2 ** (bits - 1)
            scale = jnp.clip(jnp.max(jnp.abs(jax.lax.stop_gradient(x)), axis=-1, keepdims=True), 1e-05) / pos
            q = jnp.clip(jnp.round(x / scale), -neg, pos) * scale
            return x + jax.lax.stop_gradient(q - x)

        def _ternary_quantize_ste(w):
            scale = jnp.clip(jnp.mean(jnp.abs(jax.lax.stop_gradient(w)), axis=1, keepdims=True), 1e-05)
            n = w / scale
            tern = jnp.where(n > 0.5, 1.0, jnp.where(n < -0.5, -1.0, 0.0))
            q = tern * scale
            return w + jax.lax.stop_gradient(q - w)
        key = jax.random.key(seed)
        k1, k2 = jax.random.split(key)
        x = jax.random.normal(k1, (8, 4096, IN_FEATURES), dtype=jnp.float32)
        bound = 1.0 / np.sqrt(IN_FEATURES)
        weight = jax.random.uniform(k2, (512, IN_FEATURES), dtype=jnp.float32, minval=-bound, maxval=bound)
        return {'x': x, 'weight': weight}
    _L0_ffn_all = _L0_ffn_setup()
    _L0_ffn_in = {k: v for k, v in _L0_ffn_all.items() if k in ('weight',)}
    del _L0_ffn_all

    def _L1_xattn_setup():
        import jax, jax.numpy as jnp
        import numpy as np
        NUM_HEADS = 16
        CLAMP = 10000.0
        key = jax.random.key(seed)
        ks = jax.random.split(key, 8)
        B, Nq, Nkv, Cq, Ckv = (4, 1024, 1024, 512, 384)
        s_q = 1.0 / np.sqrt(Cq)
        s_kv = 1.0 / np.sqrt(Ckv)
        return {'query': jax.random.normal(ks[0], (B, Nq, Cq), jnp.float32), 'key_value': jax.random.normal(ks[1], (B, Nkv, Ckv), jnp.float32), 'Wq': jax.random.normal(ks[2], (Cq, Cq), jnp.float32) * s_q, 'bq': jnp.zeros((Cq,), jnp.float32), 'Wk': jax.random.normal(ks[3], (Ckv, Cq), jnp.float32) * s_kv, 'bk': jnp.zeros((Cq,), jnp.float32), 'Wv': jax.random.normal(ks[4], (Ckv, Cq), jnp.float32) * s_kv, 'bv': jnp.zeros((Cq,), jnp.float32), 'Wo': jax.random.normal(ks[5], (Cq, Cq), jnp.float32) * s_q, 'bo': jnp.zeros((Cq,), jnp.float32)}
    _L1_xattn_all = _L1_xattn_setup()
    _L1_xattn_in = {k: v for k, v in _L1_xattn_all.items() if k in ('Wq', 'bq', 'Wk', 'bk', 'Wv', 'bv', 'Wo', 'bo')}
    del _L1_xattn_all

    def _L1_ffn_setup():
        import jax, jax.numpy as jnp
        import numpy as np
        EMB = 512
        FF = 4 * EMB

        def _ternary(w):
            scale = jnp.maximum(jnp.mean(jnp.abs(w)), 1e-08)
            w_t = jnp.clip(jnp.round(w / scale), -1.0, 1.0)
            return w + jax.lax.stop_gradient(w_t - w)
        key = jax.random.key(seed)
        kx, k1, k2, kb1, kb2 = jax.random.split(key, 5)
        x = jax.random.normal(kx, (4, 1024, EMB), dtype=jnp.float32)
        lim1 = 1.0 / np.sqrt(EMB)
        lim2 = 1.0 / np.sqrt(FF)
        W1 = jax.random.uniform(k1, (FF, EMB), jnp.float32, -lim1, lim1)
        b1 = jax.random.uniform(kb1, (FF,), jnp.float32, -lim1, lim1)
        W2 = jax.random.uniform(k2, (EMB, FF), jnp.float32, -lim2, lim2)
        b2 = jax.random.uniform(kb2, (EMB,), jnp.float32, -lim2, lim2)
        return {'x': x, 'W1': W1, 'b1': b1, 'W2': W2, 'b2': b2}
    _L1_ffn_all = _L1_ffn_setup()
    _L1_ffn_in = {k: v for k, v in _L1_ffn_all.items() if k in ('W1', 'b1', 'W2', 'b2')}
    del _L1_ffn_all
    return {'x': x, 'ctx_768': ctx_768, 'L0_xattn_Wq': _L0_xattn_in['Wq'], 'L0_xattn_bq': _L0_xattn_in['bq'], 'L0_xattn_Wk': _L0_xattn_in['Wk'], 'L0_xattn_bk': _L0_xattn_in['bk'], 'L0_xattn_Wv': _L0_xattn_in['Wv'], 'L0_xattn_bv': _L0_xattn_in['bv'], 'L0_xattn_Wo': _L0_xattn_in['Wo'], 'L0_xattn_bo': _L0_xattn_in['bo'], 'L0_xattn_ln_gamma': _L0_xattn_in['ln_gamma'], 'L0_xattn_ln_beta': _L0_xattn_in['ln_beta'], 'L0_ffn_weight': _L0_ffn_in['weight'], 'L1_xattn_Wq': _L1_xattn_in['Wq'], 'L1_xattn_bq': _L1_xattn_in['bq'], 'L1_xattn_Wk': _L1_xattn_in['Wk'], 'L1_xattn_bk': _L1_xattn_in['bk'], 'L1_xattn_Wv': _L1_xattn_in['Wv'], 'L1_xattn_bv': _L1_xattn_in['bv'], 'L1_xattn_Wo': _L1_xattn_in['Wo'], 'L1_xattn_bo': _L1_xattn_in['bo'], 'L1_ffn_W1': _L1_ffn_in['W1'], 'L1_ffn_b1': _L1_ffn_in['b1'], 'L1_ffn_W2': _L1_ffn_in['W2'], 'L1_ffn_b2': _L1_ffn_in['b2']}

def reference(x, ctx_768, L0_xattn_Wq, L0_xattn_bq, L0_xattn_Wk, L0_xattn_bk, L0_xattn_Wv, L0_xattn_bv, L0_xattn_Wo, L0_xattn_bo, L0_xattn_ln_gamma, L0_xattn_ln_beta, L0_ffn_weight, L1_xattn_Wq, L1_xattn_bq, L1_xattn_Wk, L1_xattn_bk, L1_xattn_Wv, L1_xattn_bv, L1_xattn_Wo, L1_xattn_bo, L1_ffn_W1, L1_ffn_b1, L1_ffn_W2, L1_ffn_b2):
    import jax
    import jax.numpy as jnp

    def _L0_xattn_ref(query, key, value, Wq, bq, Wk, bk, Wv, bv, Wo, bo, ln_gamma, ln_beta):
        import jax, jax.numpy as jnp
        import numpy as np
        QUERY_DIM, KV_DIM, EMBED_DIM, NUM_HEADS = (512, 384, 512, 16)
        HEAD_DIM = EMBED_DIM // NUM_HEADS
        SCALE = HEAD_DIM ** (-0.5)
        LN_EPS = 1e-05

        def _l2norm(x, eps=1e-12):
            n = jnp.sqrt(jnp.sum(x * x, axis=-1, keepdims=True))
            return x / jnp.maximum(n, eps)
        B, Nq, _ = query.shape
        Nk = key.shape[1]
        Qp = query @ Wq + bq
        K = _l2norm(key @ Wk + bk)
        V = value @ Wv + bv
        Q = _l2norm(Qp)
        Q = Q.reshape(B, Nq, NUM_HEADS, HEAD_DIM).transpose(0, 2, 1, 3)
        K = K.reshape(B, Nk, NUM_HEADS, HEAD_DIM).transpose(0, 2, 1, 3)
        V = V.reshape(B, Nk, NUM_HEADS, HEAD_DIM).transpose(0, 2, 1, 3)
        scores = jnp.einsum('bhqd,bhkd->bhqk', Q, K) * SCALE
        attn = jax.nn.softmax(scores, axis=-1)
        out = jnp.einsum('bhqk,bhkd->bhqd', attn, V)
        out = out.transpose(0, 2, 1, 3).reshape(B, Nq, EMBED_DIM)
        out = out @ Wo + bo
        x = out + Qp
        mu = jnp.mean(x, axis=-1, keepdims=True)
        var = jnp.mean((x - mu) ** 2, axis=-1, keepdims=True)
        return (x - mu) / jnp.sqrt(var + LN_EPS) * ln_gamma + ln_beta

    def _L0_ffn_ref(x, weight):
        import jax, jax.numpy as jnp
        import numpy as np
        IN_FEATURES = 512
        ACT_BITS = 4

        def _hadamard(size: int) -> np.ndarray:
            h = np.array([[1.0]], dtype=np.float64)
            while h.shape[0] < size:
                h = np.block([[h, h], [h, -h]])
            return (h / np.sqrt(size)).astype(np.float32)

        def _quantize_activations(x, bits=ACT_BITS):
            pos = 2 ** (bits - 1) - 1
            neg = 2 ** (bits - 1)
            scale = jnp.clip(jnp.max(jnp.abs(jax.lax.stop_gradient(x)), axis=-1, keepdims=True), 1e-05) / pos
            q = jnp.clip(jnp.round(x / scale), -neg, pos) * scale
            return x + jax.lax.stop_gradient(q - x)

        def _ternary_quantize_ste(w):
            scale = jnp.clip(jnp.mean(jnp.abs(jax.lax.stop_gradient(w)), axis=1, keepdims=True), 1e-05)
            n = w / scale
            tern = jnp.where(n > 0.5, 1.0, jnp.where(n < -0.5, -1.0, 0.0))
            q = tern * scale
            return w + jax.lax.stop_gradient(q - w)
        H = jnp.asarray(_hadamard(IN_FEATURES))
        xh = x @ H
        xq = _quantize_activations(xh)
        wq = _ternary_quantize_ste(weight)
        return jnp.einsum('bsi,oi->bso', xq, wq)

    def _L1_xattn_ref(query, key_value, Wq, bq, Wk, bk, Wv, bv, Wo, bo):
        import jax, jax.numpy as jnp
        import numpy as np
        NUM_HEADS = 16
        CLAMP = 10000.0
        B, Nq, Cq = query.shape
        Nkv = key_value.shape[1]
        H = NUM_HEADS
        D = Cq // H
        scale = D ** (-0.5)
        q = (query @ Wq + bq).reshape(B, Nq, H, D).transpose(0, 2, 1, 3)
        k = (key_value @ Wk + bk).reshape(B, Nkv, H, D).transpose(0, 2, 1, 3)
        v = (key_value @ Wv + bv).reshape(B, Nkv, H, D).transpose(0, 2, 1, 3)
        attn = jnp.einsum('bhqd,bhkd->bhqk', q, k) * scale
        attn = jnp.clip(attn, -CLAMP, CLAMP)
        attn = jax.nn.softmax(attn, axis=-1)
        attn = jnp.where(jnp.any(jnp.isnan(attn)), jnp.asarray(1.0 / Nkv, attn.dtype), attn)
        x = jnp.einsum('bhqk,bhkd->bqhd', attn, v).reshape(B, Nq, Cq)
        return x @ Wo + bo

    def _L1_ffn_ref(x, W1, b1, W2, b2):
        import jax, jax.numpy as jnp
        import numpy as np
        EMB = 512
        FF = 4 * EMB

        def _ternary(w):
            scale = jnp.maximum(jnp.mean(jnp.abs(w)), 1e-08)
            w_t = jnp.clip(jnp.round(w / scale), -1.0, 1.0)
            return w + jax.lax.stop_gradient(w_t - w)
        h = jnp.einsum('bsd,fd->bsf', x, _ternary(W1)) + b1
        h = jax.nn.gelu(h, approximate=False)
        out = jnp.einsum('bsf,df->bsd', h, _ternary(W2)) + b2
        return out
    x = x + _L0_xattn_ref(_layernorm(x, axis=-1), ctx_768, ctx_768, L0_xattn_Wq, L0_xattn_bq, L0_xattn_Wk, L0_xattn_bk, L0_xattn_Wv, L0_xattn_bv, L0_xattn_Wo, L0_xattn_bo, L0_xattn_ln_gamma, L0_xattn_ln_beta)
    x = x + _L0_ffn_ref(_layernorm(x, axis=-1), L0_ffn_weight)
    x = x + _L1_xattn_ref(_layernorm(x, axis=-1), ctx_768, L1_xattn_Wq, L1_xattn_bq, L1_xattn_Wk, L1_xattn_bk, L1_xattn_Wv, L1_xattn_bv, L1_xattn_Wo, L1_xattn_bo)
    x = x + _L1_ffn_ref(_layernorm(x, axis=-1), L1_ffn_W1, L1_ffn_b1, L1_ffn_W2, L1_ffn_b2)
    return x

_drawn_inputs = setup_inputs


def setup_inputs(seed=0):
    import zlib

    import numpy as np

    out = dict(_drawn_inputs(seed))
    spreads = {'L0_xattn_bq': (0.0, 0.1),
     'L0_xattn_bk': (0.0, 2.0),
     'L0_xattn_bv': (0.0, 0.1),
     'L0_xattn_bo': (0.0, 0.1),
     'L0_xattn_ln_gamma': (1.0, 0.2),
     'L0_xattn_ln_beta': (0.0, 0.1),
     'L1_xattn_bq': (0.0, 0.654),
     'L1_xattn_bk': (0.0, 2.0),
     'L1_xattn_bv': (0.0, 0.1),
     'L1_xattn_bo': (0.0, 0.1)}
    factors = {'L0_xattn_Wk': 64.0, 'L1_ffn_b1': 46.322, 'L1_ffn_b2': 64.0}
    for name, (base, spread) in spreads.items():
        noise = np.random.default_rng([zlib.crc32(name.encode()), seed]).standard_normal(out[name].shape)
        drawn = base * np.exp(spread * noise) if base else spread * noise
        out[name] = jnp.asarray(drawn.astype(out[name].dtype))
    for name, factor in factors.items():
        out[name] = (out[name] * factor).astype(out[name].dtype)
    return out
```

```python
from contextlib import ExitStack

import numpy as np

import concourse.bass as bass
from concourse import mybir

P = 128
F32 = mybir.dt.float32
F16 = mybir.dt.float16
I32 = mybir.dt.int32
ACT = mybir.ActivationFunctionType
ALU = mybir.AluOpType
AX_X = mybir.AxisListType.X

B, S, D, CD = 16, 256, 512, 384
H, HD = 16, 32
FF = 2048
NT = S // P
DC, CC, FC = D // P, CD // P, FF // P
EPS = 1e-5
SCALE = HD ** -0.5
CLAMP = 1e4
MAGIC = 1.5 * 2.0 ** 23
WS = 64.0
QS = 32.0
HAD = float(np.float32(1.0 / np.sqrt(D)))
QW = 3 * HD
VP = 66
OW = 33
HG = 4
GB = 2
BT = GB * NT
PREP = 8


class Signal:

    def __init__(self, sem, per_batch):
        self.sem, self.per_batch = sem, per_batch

    def at(self, b, k=None):
        return b * self.per_batch + (self.per_batch if k is None else k)


class Chain:

    def __init__(self, eng, sem):
        self.eng, self.sem, self.n, self.offset = eng, sem, 0, 0

    def __call__(self, ins):
        ins.then_inc(self.sem, 1)
        self.n += 1
        self.eng.wait_ge(self.sem, self.offset + self.n)


def pe_fills(streams):
    out = []
    for l in streams:
        out += [(("x", l, t), "T") for t in range(NT)]
        if l == 0:
            out += [(("c", t), "T") for t in range(NT)]
    for l in streams:
        out += [(("qkv", l, t, m), "J") for t in range(NT) for m in range(3)]
    for l in streams:
        out += [(("st", l, t, j, g), "T") for t in range(NT) for j in range(2) for g in range(2)]
    if 1 in streams:
        out += [(("mx", h), "J") for h in range(H)]
    for n in range(H + 3):
        for l in (0, 1):
            if l in streams and n < H:
                out.append((("s", l, n), f"S{l}"))
        for l in (0, 1):
            h = n - 2 - l
            if l in streams and 0 <= h < H and h % HG == 0:
                out.append((("o", l, h // HG), "O"))
    for l in streams:
        out += [(("ot", l, t), "T") for t in range(NT)]
        out += [(("y", l, t), "J") for t in range(NT)]
    if 0 in streams:
        for name, pool in (("xf", "T"), ("had", "J"), ("nt", "T"), ("f0", "J")):
            out += [((name, t), pool) for t in range(NT)]
    return out


POOLS = {"T": (0, 1, 4), "J": (2, 3, 7, 5, 6), "S0": (4, 1), "S1": (5, 6), "O": (2, 3, 7, 0)}


class Use:

    def __init__(self, bank, filled_at, free_at, read_at):
        self.bank, self.filled_at, self.free_at, self.read_at = bank, filled_at, free_at, read_at


def plan(streams, base, offset):
    turn = {p: 0 for p in POOLS}
    count = [[0] * 8, [0] * 8]
    uses = {}
    for name, pool in pe_fills(streams):
        n = POOLS[pool][turn[pool] % len(POOLS[pool])]
        turn[pool] += 1
        count[0][n] += pool != "O"
        count[1][n] += 1
        fills, reads = (base[k][n] + count[k][n] for k in range(2))
        if offset is None:
            uses[name] = Use(n, fills, reads - 1, reads)
        else:
            uses[name] = Use(n, offset[0][n] + fills, offset[1][n] + (reads - 1), offset[1][n] + reads)
    return uses, count


_COUNTS = {k: plan(k, [[0] * 8] * 2, None)[1] for k in ((0,), (0, 1))}


def plus(base, counts, times=1):
    return [[a + times * n for a, n in zip(x, y)] for x, y in zip(base, counts)]


def steps(eng, emit, chain=None):
    both = _COUNTS[(0, 1)]
    base = [[0] * 8] * 2
    emit((0,), 0, plan((0,), base, None)[0])
    base = plus(base, _COUNTS[(0,)])
    before = chain.n if chain else 0
    emit((0, 1), 1, plan((0, 1), base, None)[0])
    base = plus(base, both)
    per = chain.n - before if chain else 0
    with eng.Fori(2, B) as i:
        if chain:
            chain.offset = (i - 2) * per
        since = {n: (i - 2) * n for n in sorted({n for x in both for n in x})}
        emit((0, 1), i, plan((0, 1), base, [[since[n] for n in x] for x in both])[0])
    if chain:
        chain.offset = 0
        chain.n += per * (B - 3)
    base = plus(base, both, B - 2)
    emit((1,), B, plan((1,), base, None)[0])


def xattn_ffn(nc, t):
    with ExitStack() as ctx:
        def sem(name):
            return ctx.enter_context(nc.semaphore(name))

        def dram(name, shape, dt=F32):
            return nc.dram_tensor(name, shape, dt, kind="Internal").ap()

        psum = ctx.enter_context(nc.psum_tensor("psum", [P, 8, 512], F32))
        words = 49152
        arena = ctx.enter_context(nc.sbuf_tensor("arena", [P, words], F32))
        top = [0]

        def take(n):
            top[0] += n
            assert top[0] <= words, top[0]
            return arena[:, top[0] - n:top[0]]

        def bank(n):
            return psum[:, n, :]

        ident = take(P)
        identh = take(P // 2).bitcast(F16)
        had = take(2 * P).bitcast(F16)
        small = take(320)
        row_names = ["L0_xattn_bq", "L0_xattn_bk", "L0_xattn_bv", "L0_xattn_bo", "L0_xattn_ln_gamma",
                     "L0_xattn_ln_beta", "L1_xattn_bq", "L1_xattn_bk", "L1_xattn_bv", "L1_xattn_bo"]
        rows = {n: take(D) for n in row_names}
        wsc_row = take(D)
        b2_row = rows["L0_xattn_bq"]
        at_phase_b = top[0]
        tern0 = take(DC * D // 2).bitcast(F16).rearrange("p (c n) -> p c n", c=DC)
        wsplit = {}
        for l in range(2):
            for m, c in (("q", DC), ("k", CC), ("v", CC), ("o", DC)):
                wsplit[l, m] = take(c * D).bitcast(F16).rearrange("p (s c n) -> p s c n", s=2, c=c)

        def tiles(ap, n=NT):
            return ap.rearrange("p (t n) -> p t n", t=n)

        X = [tiles(take(NT * D)) for _ in range(2)]
        xn = [tiles(take(NT * D)) for _ in range(2)]
        xT_raw = [take(DC * S) for _ in range(2)]
        xT = [a.bitcast(F16).rearrange("p (s c n) -> p s c n", s=2, c=DC) for a in xT_raw]
        cT_raw = [take(CC * S) for _ in range(2)]
        cT = [a.bitcast(F16).rearrange("p (s c n) -> p s c n", s=2, c=CC) for a in cT_raw]
        qf0 = tiles(take(NT * D))
        kv0 = take(4 * D)
        qk_raw = [take(2 * NT * H * QW // 2) for _ in range(2)]
        qks = [a.bitcast(F16).rearrange("p (j t h s d) -> p j t h s d", j=2, t=NT, h=H, s=3) for a in qk_raw]

        def qk_hi_of(l, j, k):
            return qks[l][:, j, k, :, 0:3:2 - j, :] if j == 0 else qks[l][:, j, k, :, 0:2, :]

        def qk_one_hi_of(l, j, k):
            return qks[l][:, j, k, :, 0, :]

        def qk_lo_of(l, j, k):
            return qks[l][:, j, k, :, 1 + j, :]

        vs = [take(NT * H * VP // 2).bitcast(F16).rearrange("p (t h d) -> p t h d", t=NT, h=H) for _ in range(2)]
        qkT_raw = [take(2 * H * S // 2) for _ in range(2)]
        qkT = [a.bitcast(F16).rearrange("p (j h n) -> p j h n", j=2, h=H) for a in qkT_raw]
        kv1 = qkT_raw[1][:, H * S - 3 * D:H * S]
        end_a = top[0]
        kf0 = [kv0[:, 0:D], kv0[:, D:2 * D]]
        vf0 = [kv0[:, 2 * D:3 * D], kv0[:, 3 * D:4 * D]]
        CT = tiles(kv0[:, 2 * D:2 * D + NT * CD])
        tq = kf0
        yf = vf0
        pf = [vf0, [xT_raw[1][:, 0:D], xT_raw[1][:, D:2 * D]]]
        xp = qf0
        NP = 3
        ph = [qk_raw[l][:, 0:NP * D // 2].bitcast(F16).rearrange("p (r n) -> p r n", r=NP) for l in range(2)]
        pl = [qk_raw[l][:, NP * D // 2:NP * D].bitcast(F16).rearrange("p (r n) -> p r n", r=NP) for l in range(2)]
        nq = tiles(qk_raw[0][:, 0:NT * D // 2].bitcast(F16))
        nT = qk_raw[0][:, NT * D // 2:NT * D].bitcast(F16).rearrange("p (c n) -> p c n", c=DC)

        sm = [0]

        def tiny(n):
            sm[0] += n
            return small[:, sm[0] - n:sm[0]]

        magic = tiny(1)
        half4 = tiny(4)
        eps4, qs4, had4 = tiny(4), tiny(4), tiny(4)
        one4 = tiny(4)
        st = tiny(6 * 4)
        mv = {k: tiny(2 * 4).rearrange("p (t k) -> p t k", k=2) for k in ("A0", "A1", "E", "F", "B")}
        rs = {k: tiny(4) for k in ("A0", "A1", "E", "F", "B")}
        tmp = {k: tiny(4) for k in ("A0", "A1", "E", "F", "B", "N", "Q")}
        ssq = tiny(4)
        rn = tiny(4)
        am = tiny(NT)
        qsc = tiny(NT)
        qrs = tiny(NT)
        mx = tiny(NT * H).rearrange("p (t h) -> p t h", t=NT)
        mneg = tiny(NT * H // 2).bitcast(F16).rearrange("p (t h) -> p t h", t=NT)
        rden = [tiny(NT * HG).rearrange("p (t h) -> p t h", t=NT) for _ in range(2)]
        wab = tiny(FC)
        wsum = tiny(2)
        wthr = tiny(8)
        wsum_rows = tiny(DC)
        one_col = tiny(1)

        top[0] = at_phase_b
        b1c = take(FC)
        w1T = take(DC * FF // 2).bitcast(F16).rearrange("p (c f) -> p c f", c=DC)
        w2T = take(FC * D // 2).bitcast(F16).rearrange("p (c n) -> p c n", c=FC)
        b_top = top[0]
        wst = take(FC * D)
        wgt = take(FC * D // 2).bitcast(F16)
        wtern = take(FC * D // 2).bitcast(F16)
        top[0] = b_top
        Xb = [tiles(take(BT * D), BT) for _ in range(2)]
        xnb = tiles(take(BT * D), BT)
        xTb = take(DC * BT * P).bitcast(F16).rearrange("p (s c n) -> p s c n", s=2, c=DC)
        gf = [take(BT * P) for _ in range(2)]
        NG = 4
        gh = take(NG * BT * P // 2).bitcast(F16).rearrange("p (r n) -> p r n", r=NG)
        gl = take(NG * BT * P // 2).bitcast(F16).rearrange("p (r n) -> p r n", r=NG)

        xd = t["x"].rearrange("b (t p) d -> b p t d", p=P)
        cd = t["ctx_768"].rearrange("b (t p) d -> b p t d", p=P)
        od = t["out"].rearrange("b (t p) d -> b p t d", p=P)
        x1d = dram("x1_scratch", [B, P, NT * D]).rearrange("b p (t d) -> b p t d", t=NT)
        x2d = dram("x2_scratch", [B, P, NT * D]).rearrange("b p (t d) -> b p t d", t=NT)

        def batch(d, b):
            return d[b] if isinstance(b, int) else d[bass.ds(b, 1)].rearrange("a p t d -> p (a t) d")

        filled = [sem(f"bank{n}_filled") for n in range(8)]
        read = [sem(f"bank{n}_read") for n in range(8)]
        CONSTS = 13
        const_ready = sem("const_ready")
        consts_loaded = sem("consts_loaded")
        w_loaded = [sem(f"w_loaded{n}") for n in range(2)]
        w_split = sem("w_split")
        w_hi = sem("w_hi")
        setup_pe = sem("setup_pe")
        setup_dve = sem("setup_dve")
        setup_act = sem("setup_act")
        setup_pool = sem("setup_pool")
        dve_step, pool_step = sem("dve_step"), sem("pool_step")

        def signals(name, *per_batch):
            return [Signal(sem(f"{name}_{l}"), k) for l, k in enumerate(per_batch)]

        x_loaded = signals("x_loaded", 16, 16)
        ctx_loaded = Signal(sem("ctx_loaded"), 16)
        ctxT_copied = Signal(sem("ctxT_copied"), 16)
        x1_stored = Signal(sem("x1_stored"), 16)
        x2_stored = Signal(sem("x2_stored"), 16)
        stats_A = signals("statsA", 2, 2)
        rstd_A = signals("rstdA", 1, 1)
        xn_ready = signals("xn_ready", 2, 2)
        xT_hi = signals("xT_hi", NT, NT)
        ctxT_hi = Signal(sem("ctxT_hi"), NT)
        oT_hi = signals("oT_hi", NT, NT)
        xbias = signals("xbias", 1, 1)
        squares = Signal(sem("squares"), 4)
        guarded = Signal(sem("guarded"), 1)
        norms = Signal(sem("norms"), 1)
        qk_hi = signals("qk_hi", 4, 4)
        qk_lo = signals("qk_lo", 4, 4)
        v_hi = signals("v_hi", NT, NT)
        v_lo = signals("v_lo", NT, NT)
        shift_ready = Signal(sem("shift_ready"), 1)
        clipped = Signal(sem("clipped"), H)
        shifted = Signal(sem("shifted"), H)
        p_hi = signals("p_hi", H, H)
        lo_on_dve = [[h % 2 == 1 for h in range(H)], [False] * H]
        p_lo_dve = signals("p_lo_dve", *[sum(x) for x in lo_on_dve])
        p_lo_pool = signals("p_lo_pool", *[H - sum(x) for x in lo_on_dve])
        av_done = signals("av_done", H, H)
        qf_biased = Signal(sem("qf_biased"), 1)
        stats_E = Signal(sem("statsE"), 2)
        rstd_E = Signal(sem("rstdE"), 2)
        xp_ready = Signal(sem("xp_ready"), 2)
        stats_F = Signal(sem("statsF"), 2)
        rstd_F = Signal(sem("rstdF"), 2)
        xnF_ready = Signal(sem("xnF_ready"), 2)
        xF_hi = Signal(sem("xF_hi"), 2)
        absmax = Signal(sem("absmax"), 2)
        qscale = Signal(sem("qscale"), 2)
        nq_ready = Signal(sem("nq_ready"), 2)
        x1_ready = Signal(sem("x1_ready"), 2)

        wb_loaded = sem("wb_loaded")
        wb_part, wb_sum, wb_tern = sem("wb_part"), sem("wb_sum"), sem("wb_tern")
        wtr_filled, wtr_read = sem("wtr_filled"), sem("wtr_read")
        xb_loaded = [sem(f"xb_loaded{n}") for n in range(2)]
        statsB, rstdB, xnb_ready, xb_biased = sem("statsB"), sem("rstdB"), sem("xnb_ready"), sem("xb_biased")
        xTb_filled, xTb_hi, xTb_read = sem("xTb_filled"), sem("xTb_hi"), sem("xTb_read")
        h_filled, gelu_done, g_hi = sem("h_filled"), sem("gelu_done"), sem("g_hi")
        g_lo = [sem("g_lo_pool"), sem("g_lo_dve")]
        g_used, yb_ready, yb_stored = sem("g_used"), sem("yb_ready"), sem("yb_stored")

        def later(eng, s, value):
            if not isinstance(value, int) or value > 0:
                eng.wait_ge(s, value)

        def g_lo_wait(eng, s, f):
            later(eng, g_lo[f % 2], s * (FC // 2) + f // 2 + 1)

        def steps_b(step_b, eng, chain=None):
            pairs = B // GB // 2
            per = 0
            for slot in range(2):
                n = chain.n if chain else 0
                step_b(slot, slot, 0, True)
                per += chain.n - n if chain else 0
            with eng.Fori(1, pairs - 1) as r:
                if chain:
                    chain.offset = (r - 1) * per
                for slot in range(2):
                    step_b(2 * r + slot, slot, r, True)
            if chain:
                chain.offset = 0
                chain.n += per * (pairs - 3)
            for slot in range(2):
                step_b(2 * (pairs - 1) + slot, slot, pairs - 1, slot == 0)

        def all_read(eng, uses):
            for u in {u.bank: u for u in uses}.values():
                eng.wait_ge(read[u.bank], u.read_at)

        def heads(ap):
            return ap.rearrange("p (h d) -> p h d", h=H)

        block = ctx.enter_context(nc.Block())
        W = [(l, m) for l in range(2) for m in "qkvo"]
        stage_w = [take_w.rearrange("p (c n) -> p c n", c=DC) for take_w in (
            arena[:, end_a - 4096:end_a - 2048], arena[:, end_a - 2048:end_a])]
        gt0 = arena[:, end_a - 6144:end_a - 5120].bitcast(F16).rearrange("p (c n) -> p c n", c=DC)
        tr0 = arena[:, end_a - 5120:end_a - 4096].bitcast(F16).rearrange("p (c n) -> p c n", c=DC)

        @block.sync
        def _(sp):
            for n in row_names:
                sp.dma_start(rows[n], t[n].rearrange("(a n) -> a n", a=1).broadcast_to([P, D])).then_inc(consts_loaded, 16)
            sp.dma_start(had, t["signs"]).then_inc(consts_loaded, 16)
            for n, (l, m) in enumerate(W):
                if n >= 2:
                    sp.wait_ge(w_split, n - 1)
                w = t[f"L{l}_xattn_W{m}"].rearrange("(c p) n -> p c n", p=P)
                sp.dma_start(stage_w[n % 2][:, 0:w.shape[1], :], w).then_inc(w_loaded[n % 2], 16)
            sp.wait_ge(w_split, len(W) - 1)
            sp.dma_start(stage_w[0], t["L0_ffn_weight"].rearrange("(c p) n -> p c n", p=P)).then_inc(w_loaded[0], 16)

            def step(streams, i, use):
                b0, b1 = i, i - 1
                if 0 in streams:
                    if not (isinstance(i, int) and i == 0):
                        sp.wait_ge(xp_ready.sem, xp_ready.at(b0 - 1))
                    else:
                        sp.wait_ge(setup_dve, 3)
                    sp.dma_start(X[0], batch(xd, b0)).then_inc(x_loaded[0].sem, 16)
                    sp.dma_start(CT, batch(cd, b0)).then_inc(ctx_loaded.sem, 16)
                if 1 in streams:
                    if not (isinstance(i, int) and i == 1):
                        sp.wait_ge(x2_stored.sem, x2_stored.at(b1 - 1))
                    sp.wait_ge(x1_stored.sem, x1_stored.at(b1))
                    sp.dma_start(X[1], batch(x1d, b1)).then_inc(x_loaded[1].sem, 16)
                if 0 in streams:
                    for k in range(NT):
                        sp.wait_ge(read[use["c", k].bank], use["c", k].read_at)
                    if 1 in streams:
                        u = use["qkv", 1, NT - 1, 2]
                        sp.wait_ge(filled[u.bank], u.filled_at)
                    sp.dma_start(cT_raw[1], cT_raw[0]).then_inc(ctxT_copied.sem, 16)
                if 1 in streams:
                    for k in range(NT):
                        sp.wait_ge(read[use["y", 1, k].bank], use["y", 1, k].read_at)
                    sp.dma_start(batch(x2d, b1), X[1]).then_inc(x2_stored.sem, 16)

            steps(sp, step)

            sp.wait_ge(x2_stored.sem, x2_stored.at(B - 1))
            w1 = t["L1_ffn_W1"].rearrange("(c p) n -> p c n", p=P)
            sp.dma_start(wst.rearrange("p (c n) -> p c n", c=FC), w1).then_inc(wb_loaded, 16)
            sp.dma_start(b2_row, t["L1_ffn_b2"].rearrange("(a n) -> a n", a=1).broadcast_to([P, D])).then_inc(wb_loaded, 16)
            sp.dma_start(b1c, t["L1_ffn_b1"].rearrange("(c p) -> p c", p=P),
                         allow_slow_non_contiguous=True).then_inc(wb_loaded, 16)
            sp.wait_ge(wb_tern, 1)
            w2 = t["L1_ffn_W2"].rearrange("(c p) n -> p c n", p=P)
            sp.dma_start(wst.rearrange("p (c n) -> p c n", c=DC), w2).then_inc(wb_loaded, 16)
            sp.wait_ge(wtr_read, 16)

            def load(s, slot):
                for g in range(GB):
                    sp.dma_start(Xb[slot][:, g * NT:(g + 1) * NT, :], batch(x2d, s * GB + g)).then_inc(xb_loaded[slot], 16)

            def store(s, slot):
                sp.wait_ge(yb_ready, s * BT + BT)
                for g in range(GB):
                    sp.dma_start(batch(od, s * GB + g), Xb[slot][:, g * NT:(g + 1) * NT, :]).then_inc(yb_stored, 16)

            load(0, 0)
            load(1, 1)
            with sp.Fori(0, B // GB // 2 - 1) as r:
                for slot in range(2):
                    s = 2 * r + slot
                    store(s, slot)
                    sp.wait_ge(yb_stored, s * (16 * GB) + 16 * GB)
                    load(s + 2, slot)
            for slot in range(2):
                store(B // GB - 2 + slot, slot)
            sp.wait_ge(yb_stored, 16 * B)

        @block.gpsimd
        def _(pool):
            chain = Chain(pool, pool_step)
            gp = nc.gpsimd
            gp.memset(ident, 0.0).then_inc(const_ready, 1)
            gp.memset(identh, 0.0).then_inc(const_ready, 1)
            pool.wait_ge(const_ready, 2)
            for m in (ident, identh):
                gp.affine_select(out=m, in_=m, compare_op=ALU.not_equal, fill=1.0, base=0,
                                 pattern=[[-1, P]], channel_multiplier=1).then_inc(const_ready, 1)
            for ap, value in ((half4, -0.5), (eps4, EPS), (qs4, QS), (had4, HAD)):
                gp.memset(ap, value).then_inc(const_ready, 1)
            gp.memset(one4, -1.0).then_inc(const_ready, 1)
            gp.memset(magic, MAGIC).then_inc(const_ready, 1)
            gp.memset(one_col, 1.0).then_inc(const_ready, 1)
            for l in range(2):
                gp.memset(vs[l][:, :, :, HD:HD + 2], 1.0).then_inc(const_ready, 1)
            pool.wait_ge(const_ready, CONSTS)
            pool.wait_ge(consts_loaded, 16 * (len(row_names) + 1))

            def rstd(name, ts):
                at = slice(ts[0], ts[0] + len(ts))
                chain(gp.tensor_tensor(tmp[name][:, at], mv[name][:, at, 1], eps4[:, at], ALU.add))
                return gp.tensor_tensor(rs[name][:, at], tmp[name][:, at], half4[:, at], ALU.pow)

            def step(streams, i, use):
                bs = {0: i, 1: i - 1}
                for l in streams:
                    b = bs[l]
                    pool.wait_ge(stats_A[l].sem, stats_A[l].at(b))
                    rstd(f"A{l}", [0, 1]).then_inc(rstd_A[l].sem, 1)
                    pool.wait_ge(xn_ready[l].sem, xn_ready[l].at(b))
                    bias = rows["L0_xattn_ln_beta" if l == 0 else "L1_xattn_bo"]
                    gp.tensor_tensor(X[l], X[l], bias.unsqueeze(1).to_broadcast([P, NT, D]), ALU.add).then_inc(xbias[l].sem, 1)
                for l in streams:
                    b = bs[l]
                    vf = vf0 if l == 0 else [kv1[:, 2 * D:3 * D]] * 2
                    if l == 0:
                        pool.wait_ge(guarded.sem, guarded.at(b))
                        chain(gp.tensor_tensor(tmp["N"], ssq, half4, ALU.pow))
                        gp.tensor_tensor(rn, tmp["N"], qs4, ALU.mult).then_inc(norms.sem, 1)
                    for k in range(NT):
                        pool.wait_ge(v_hi[l].sem, v_hi[l].at(b, k + 1))
                        gp.tensor_tensor(vs[l][:, k, :, HD + 2:VP], heads(vf[k]), vs[l][:, k, :, 0:HD],
                                         ALU.subtract).then_inc(v_lo[l].sem, 1)
                    if l == 0:
                        pool.wait_ge(qk_hi[0].sem, qk_hi[0].at(b))
                        pool.wait_ge(qk_lo[0].sem, qk_lo[0].at(b))
                        gp.tensor_tensor(qf0, qf0, rows["L0_xattn_bo"].unsqueeze(1).to_broadcast([P, NT, D]),
                                         ALU.add).then_inc(qf_biased.sem, 1)
                for n in range(H + 1):
                    for l, h in ((1, n - 1), (0, n)):
                        if l in streams and 0 <= h < H and not lo_on_dve[l][h]:
                            b = bs[l]
                            pool.wait_ge(p_hi[l].sem, p_hi[l].at(b, h + 1))
                            if h >= NP:
                                pool.wait_ge(av_done[l].sem, av_done[l].at(b, h + 1 - NP))
                            gp.tensor_tensor(pl[l][:, h % NP, :], pf[l][h % 2], ph[l][:, h % NP, :],
                                             ALU.subtract).then_inc(p_lo_pool[l].sem, 1)
                if 0 in streams:
                    b = i
                    for k in range(NT):
                        pool.wait_ge(stats_E.sem, stats_E.at(b, k + 1))
                        rstd("E", [k]).then_inc(rstd_E.sem, 1)
                    for k in range(NT):
                        pool.wait_ge(stats_F.sem, stats_F.at(b, k + 1))
                        rstd("F", [k]).then_inc(rstd_F.sem, 1)
                    for k in range(NT):
                        pool.wait_ge(absmax.sem, absmax.at(b, k + 1))
                        chain(gp.tensor_tensor(tmp["Q"][:, k:k + 1], qsc[:, k:k + 1], one4[:, 0:1], ALU.pow))
                        gp.tensor_tensor(qrs[:, k:k + 1], tmp["Q"][:, k:k + 1], had4[:, 0:1], ALU.mult).then_inc(qscale.sem, 1)
                    for k in range(NT):
                        u = use["f0", k]
                        pool.wait_ge(read[u.bank], u.read_at)
                        gp.tensor_tensor(tq[k], tq[k], xp[:, k, :], ALU.add).then_inc(x1_ready.sem, 1)

            steps(pool, step, chain)

            def prep_b(s, slot):
                pool.wait_ge(statsB, s * BT + BT)
                chain(gp.tensor_tensor(tmp["B"], mv["B"][:, :, 1], eps4, ALU.add))
                gp.tensor_tensor(rs["B"], tmp["B"], half4, ALU.pow).then_inc(rstdB, 1)
                pool.wait_ge(xnb_ready, s * BT + BT)
                gp.tensor_tensor(Xb[slot], Xb[slot], b2_row.unsqueeze(1).to_broadcast([P, BT, D]), ALU.add).then_inc(xb_biased, 1)

            def step_b(s, slot, r, has_next):
                for f in range(FC):
                    if f % 2 == 0:
                        pool.wait_ge(g_hi, s * FC + f + 1)
                        gp.tensor_tensor(gl[:, f % NG, :], gf[f % 2], gh[:, f % NG, :], ALU.subtract).then_inc(g_lo[0], 1)
                    if f == PREP and has_next:
                        prep_b(s + 1, 1 - slot)

            prep_b(0, 0)
            steps_b(step_b, pool, chain)

        @block.scalar
        def _(act):
            sc = nc.scalar
            act.wait_ge(const_ready, CONSTS)
            for n, (l, m) in enumerate(W):
                c = wsplit[l, m].shape[2]
                act.wait_ge(w_loaded[n % 2], 16 * (n // 2 + 1))
                sc.activation(wsplit[l, m][:, 0], stage_w[n % 2][:, 0:c, :], ACT.Copy, scale=WS).then_inc(w_hi, 1)
            for c in range(DC):
                act.wait_ge(setup_pe, c + 2)
                sc.activation(tern0[:, c, :], bank(c + 1).bitcast(F16)[:, 0:D], ACT.Copy).then_inc(setup_act, 1)
            act.wait_ge(setup_pe, 1)
            sc.activation(wsc_row, bank(0), ACT.Copy).then_inc(setup_act, 1)
            act.wait_ge(setup_act, DC + 1)

            def twice(ap):
                return heads(ap).unsqueeze(2).to_broadcast([P, H, 2, HD])

            def hi(src_use, dst, sig, extra=()):
                act.wait_ge(filled[src_use.bank], src_use.filled_at)
                n = dst.shape[1]
                sc.activation(dst, bank(src_use.bank)[:, 0:n * P].rearrange("p (c n) -> p c n", c=n), ACT.Copy).then_inc(sig, 1)

            def step(streams, i, use):
                bs = {0: i, 1: i - 1}
                for l in streams:
                    for k in range(NT):
                        hi(use["x", l, k], xT[l][:, 0, :, k * P:(k + 1) * P], xT_hi[l].sem)
                    if l == 0:
                        if not (isinstance(i, int) and i == 0):
                            act.wait_ge(ctxT_copied.sem, ctxT_copied.at(i - 1))
                        for k in range(NT):
                            hi(use["c", k], cT[0][:, 0, :, k * P:(k + 1) * P], ctxT_hi.sem)
                for l in streams:
                    b = bs[l]
                    if l == 0:
                        for k in range(NT):
                            for j, src in enumerate((qf0[:, k, :], kf0[k])):
                                u = use["qkv", 0, k, j]
                                act.wait_ge(read[u.bank], u.read_at)
                                if j + 2 * k:
                                    act.wait_ge(squares.sem, squares.at(b, 2 * k + j))
                                sc.activation(xn[0][:, 0, :], src, ACT.Square, accum_out=ssq[:, 2 * k + j:2 * k + j + 1]).then_inc(squares.sem, 1)
                        act.wait_ge(norms.sem, norms.at(b))
                    for k in range(NT):
                        for j in range(2):
                            if l == 0:
                                src = (qf0[:, k, :], kf0[k])[j]
                                sc.activation(qk_hi_of(0, j, k), twice(src), ACT.Copy, scale=rn[:, 2 * k + j:2 * k + j + 1]).then_inc(qk_hi[0].sem, 1)
                            else:
                                u = use["qkv", 1, k, j]
                                act.wait_ge(read[u.bank], u.read_at)
                                sc.activation(qk_hi_of(1, j, k), twice(kv1[:, j * D:(j + 1) * D]), ACT.Copy).then_inc(qk_hi[1].sem, 1)
                for l in streams:
                    if l == 1:
                        act.wait_ge(qk_lo[1].sem, qk_lo[1].at(bs[1]))
                        act.wait_ge(v_lo[1].sem, v_lo[1].at(bs[1]))
                    for k in range(NT):
                        for j in range(2):
                            for g in range(2):
                                u = use["st", l, k, j, g]
                                act.wait_ge(filled[u.bank], u.filled_at)
                                sc.activation(qkT[l][0:QW, j, g * 8:(g + 1) * 8, k * P:(k + 1) * P],
                                              bank(u.bank).bitcast(F16)[0:QW].rearrange("p (h n) -> p h n", h=8),
                                              ACT.Copy).then_inc(read[u.bank], 1)
                for n in range(H + 1):
                    for l, h in ((1, n - 1), (0, n)):
                        if l not in streams or not 0 <= h < H:
                            continue
                        b = bs[l]
                        u = use["s", l, h]
                        if l == 0:
                            act.wait_ge(filled[u.bank], u.filled_at)
                            if h == 0:
                                act.wait_ge(v_lo[0].sem, v_lo[0].at(b))
                        else:
                            act.wait_ge(shifted.sem, shifted.at(b, h + 1))
                        if h >= 2:
                            lo_wait(act, l, b, h - 2)
                        sc.activation(pf[l][h % 2], bank(u.bank), ACT.Exp,
                                      scale=SCALE / (QS * QS) if l == 0 else SCALE).then_inc(read[u.bank], 1)
                for l in streams:
                    for k in range(NT):
                        hi(use["ot", l, k], xT[l][:, 0, :, k * P:(k + 1) * P], oT_hi[l].sem)
                if 0 in streams:
                    b = i
                    for k in range(NT):
                        hi(use["xf", k], xT[0][:, 0, :, k * P:(k + 1) * P], xF_hi.sem)
                    for k in range(NT):
                        act.wait_ge(qscale.sem, qscale.at(b, k + 1))
                        u = use["had", k]
                        sc.activation(tq[k], bank(u.bank), ACT.Identity, bias=magic, scale=qrs[:, k:k + 1]).then_inc(read[u.bank], 1)
                    for k in range(NT):
                        u = use["nt", k]
                        act.wait_ge(filled[u.bank], u.filled_at)
                        sc.activation(nT[:, :, k * P:(k + 1) * P],
                                      bank(u.bank).bitcast(F16)[:, 0:D].rearrange("p (c n) -> p c n", c=DC),
                                      ACT.Copy).then_inc(read[u.bank], 1)
                    act.wait_ge(x1_ready.sem, x1_ready.at(b))
                    act.dma_start(batch(x1d, b), kv0[:, 0:2 * D].rearrange("p (t n) -> p t n", t=NT)).then_inc(x1_stored.sem, 16)

            def lo_wait(eng, l, b, h):
                if lo_on_dve[l][h]:
                    eng.wait_ge(p_lo_dve[l].sem, p_lo_dve[l].at(b, sum(lo_on_dve[l][:h + 1])))
                else:
                    eng.wait_ge(p_lo_pool[l].sem, p_lo_pool[l].at(b, h + 1 - sum(lo_on_dve[l][:h + 1])))

            steps(act, step)

            for w, dst in ((0, w1T), (1, w2T)):
                for g in range(DC * FC // 8):
                    act.wait_ge(wtr_filled, w * 8 + g + 1)
                    src = bank(g % 4).bitcast(F16)
                    if w == 0:
                        out = dst[:, g % DC, (g // DC) * 8 * P:(g // DC + 1) * 8 * P]
                        sc.activation(out, src, ACT.Copy).then_inc(wtr_read, 1)
                    else:
                        out = dst[:, (g // 4) * 8:(g // 4 + 1) * 8, (g % 4) * P:(g % 4 + 1) * P]
                        sc.activation(out, src.rearrange("p (c n) -> p c n", c=8), ACT.Copy).then_inc(wtr_read, 1)
            act.wait_ge(wb_loaded, 64)

            def prep_b(s):
                for k in range(BT):
                    act.wait_ge(xTb_filled, s * BT + k + 1)
                    sc.activation(xTb[:, 0, :, k * P:(k + 1) * P], bank(6 + k % 2).rearrange("p (c n) -> p c n", c=DC),
                                  ACT.Copy).then_inc(xTb_hi, 1)

            def step_b(s, slot, r, has_next):
                for f in range(FC):
                    act.wait_ge(h_filled, s * FC + f + 1)
                    g_lo_wait(act, s, f - 2)
                    sc.activation(gf[f % 2], bank(4 + f % 2), ACT.Gelu, bias=b1c[:, f:f + 1]).then_inc(gelu_done, 1)
                if has_next:
                    prep_b(s + 1)

            prep_b(0)
            steps_b(step_b, act)

        @block.vector
        def _(dve):
            chain = Chain(dve, dve_step)
            v = nc.vector
            dve.wait_ge(const_ready, CONSTS)
            dve.wait_ge(consts_loaded, 16 * (len(row_names) + 1))
            for n, (l, m) in enumerate(W):
                c = wsplit[l, m].shape[2]
                dve.wait_ge(w_hi, n + 1)
                v.scalar_tensor_tensor(out=wsplit[l, m][:, 1], in0=stage_w[n % 2][:, 0:c, :], scalar=WS,
                                       in1=wsplit[l, m][:, 0], op0=ALU.mult, op1=ALU.subtract).then_inc(w_split, 1)
            dve.wait_ge(w_loaded[0], 16 * (len(W) // 2 + 1))
            chain(v.tensor_reduce(wthr[:, 0:DC], stage_w[0], AX_X, ALU.add, apply_absolute_value=True))
            chain(v.tensor_scalar(wsum_rows, wthr[:, 0:DC], 1.0 / D, 1e-5, ALU.mult, ALU.max))
            v.tensor_scalar(wthr[:, 0:DC], wsum_rows, 0.5, None, ALU.mult).then_inc(setup_dve, 1)
            v.tensor_scalar(wthr[:, DC:2 * DC], wsum_rows, -0.5, None, ALU.mult).then_inc(setup_dve, 1)
            dve.wait_ge(setup_dve, 2)
            for c in range(DC):
                v.tensor_scalar(gt0[:, c, :], stage_w[0][:, c, :], wthr[:, DC + c:DC + c + 1], None, ALU.is_lt).then_inc(dve_step, 1)
                chain.n += 1
            dve.wait_ge(dve_step, chain.n)
            for c in range(DC):
                ins = v.scalar_tensor_tensor(out=tr0[:, c, :], in0=stage_w[0][:, c, :], scalar=wthr[:, c:c + 1],
                                             in1=gt0[:, c, :], op0=ALU.is_gt, op1=ALU.subtract)
                if c < DC - 1:
                    chain(ins)
            ins.then_inc(setup_dve, 1)
            dve.wait_ge(setup_act, DC + 1)

            def ln_stats(name, src, k, sig):
                v.bn_stats(st[:, 6 * k:6 * k + 6], src)
                dve.drain()
                v.bn_aggr(mv[name][:, k, :], st[:, 6 * k:6 * k + 6]).then_inc(sig, 1)

            def normalise(name, dst, src, k, sig):
                v.tensor_scalar(dst, src, mv[name][:, k, 0:1], rs[name][:, k:k + 1], ALU.subtract, ALU.mult).then_inc(sig, 1)

            def lo(u, dst, upper, hi_sig, value):
                dve.wait_ge(hi_sig, value)
                n = dst.shape[1]
                v.tensor_tensor(dst, bank(u.bank)[:, 0:n * P].rearrange("p (c n) -> p c n", c=n), upper,
                                ALU.subtract).then_inc(read[u.bank], 1)

            def step(streams, i, use):
                bs = {0: i, 1: i - 1}
                first = isinstance(i, int) and i == 0

                def cols(a, s, k):
                    return a[:, s, :, k * P:(k + 1) * P]

                for l in streams:
                    b = bs[l]
                    dve.wait_ge(x_loaded[l].sem, x_loaded[l].at(b))
                    for k in range(NT):
                        ln_stats(f"A{l}", X[l][:, k, :], k, stats_A[l].sem)
                    dve.wait_ge(rstd_A[l].sem, rstd_A[l].at(b))
                    dve.wait_ge(stats_A[l].sem, stats_A[l].at(b))
                    for k in range(NT):
                        normalise(f"A{l}", xn[l][:, k, :], X[l][:, k, :], k, xn_ready[l].sem)
                for l in streams:
                    b = bs[l]
                    for k in range(NT):
                        lo(use["x", l, k], cols(xT[l], 1, k), cols(xT[l], 0, k), xT_hi[l].sem, xT_hi[l].at(b, k + 1))
                    if l == 0:
                        if not first:
                            dve.wait_ge(ctxT_copied.sem, ctxT_copied.at(i - 1))
                        for k in range(NT):
                            lo(use["c", k], cols(cT[0], 1, k), cols(cT[0], 0, k), ctxT_hi.sem, ctxT_hi.at(i, k + 1))
                for l in streams:
                    b = bs[l]
                    if l == 0 and not first:
                        dve.wait_ge(x1_stored.sem, x1_stored.at(i - 1))
                    for k in range(NT):
                        for j, m in enumerate("qkv"):
                            u = use["qkv", l, k, j]
                            if l == 0:
                                dst = (qf0[:, k, :], kf0[k], vf0[k])[j]
                            else:
                                dst = kv1[:, j * D:(j + 1) * D]
                                if k:
                                    if j < 2:
                                        dve.wait_ge(qk_lo[1].sem, qk_lo[1].at(b, 2 * (k - 1) + j + 1))
                                    else:
                                        dve.wait_ge(v_lo[1].sem, v_lo[1].at(b, k))
                            dve.wait_ge(filled[u.bank], u.filled_at)
                            v.scalar_tensor_tensor(out=dst, in0=bank(u.bank), scalar=1.0 / WS, in1=rows[f"L{l}_xattn_b{m}"],
                                                   op0=ALU.mult, op1=ALU.add).then_inc(read[u.bank], 1)
                            if j == 2:
                                dve.wait_ge(read[u.bank], u.read_at)
                                v.tensor_copy(vs[l][:, k, :, 0:HD], heads(dst)).then_inc(v_hi[l].sem, 1)
                        if l == 1:
                            for j in range(2):
                                dve.wait_ge(qk_hi[1].sem, qk_hi[1].at(b, 2 * k + j + 1))
                                v.tensor_tensor(qk_lo_of(1, j, k), heads(kv1[:, j * D:(j + 1) * D]),
                                                qk_one_hi_of(1, j, k), ALU.subtract).then_inc(qk_lo[1].sem, 1)
                    if l == 0:
                        dve.wait_ge(squares.sem, squares.at(b))
                        v.tensor_scalar(ssq, ssq, 1e-24, None, ALU.max).then_inc(guarded.sem, 1)
                        for k in range(NT):
                            for j in range(2):
                                dve.wait_ge(qk_hi[0].sem, qk_hi[0].at(b, 2 * k + j + 1))
                                src = (qf0[:, k, :], kf0[k])[j]
                                v.scalar_tensor_tensor(out=qk_lo_of(0, j, k), in0=heads(src),
                                                       scalar=rn[:, 2 * k + j:2 * k + j + 1], in1=qk_one_hi_of(0, j, k),
                                                       op0=ALU.mult, op1=ALU.subtract).then_inc(qk_lo[0].sem, 1)
                if 1 in streams:
                    for h in range(H):
                        u = use["mx", h]
                        dve.wait_ge(filled[u.bank], u.filled_at)
                        v.tensor_reduce(mx[:, :, h], bank(u.bank).rearrange("p (t n) -> p t n", t=NT), AX_X,
                                        ALU.max).then_inc(read[u.bank], 1)
                    dve.wait_ge(read[u.bank], u.read_at)
                    chain(v.tensor_scalar(mx, mx, CLAMP / SCALE, -CLAMP / SCALE, ALU.min, ALU.max))
                    v.tensor_scalar(mneg, mx, -1.0, None, ALU.mult).then_inc(shift_ready.sem, 1)
                for n in range(H + 4):
                    if 1 in streams and n < H:
                        u = use["s", 1, n]
                        dve.wait_ge(filled[u.bank], u.filled_at)
                        v.tensor_scalar(bank(u.bank), bank(u.bank), CLAMP / SCALE, -CLAMP / SCALE, ALU.min,
                                        ALU.max).then_inc(clipped.sem, 1)
                    for l, h in ((1, n - 1), (0, n)):
                        if l not in streams or not 0 <= h < H:
                            continue
                        b = bs[l]
                        u = use["s", l, h]
                        dve.wait_ge(read[u.bank], u.read_at)
                        if h >= NP:
                            dve.wait_ge(av_done[l].sem, av_done[l].at(b, h + 1 - NP))
                        v.tensor_copy(ph[l][:, h % NP, :], pf[l][h % 2]).then_inc(p_hi[l].sem, 1)
                        if lo_on_dve[l][h]:
                            dve.wait_ge(p_hi[l].sem, p_hi[l].at(b, h + 1))
                            v.tensor_tensor(pl[l][:, h % NP, :], pf[l][h % 2], ph[l][:, h % NP, :],
                                            ALU.subtract).then_inc(p_lo_dve[l].sem, 1)
                    for l in streams:
                        h = n - 3 - l
                        if 0 <= h < H and h % HG == HG - 1:
                            attn_out(l, bs[l], h // HG, use["o", l, h // HG])
                for l in streams:
                    b = bs[l]
                    for k in range(NT):
                        lo(use["ot", l, k], cols(xT[l], 1, k), cols(xT[l], 0, k), oT_hi[l].sem, oT_hi[l].at(b, k + 1))
                for l in streams:
                    b = bs[l]
                    dve.wait_ge(xbias[l].sem, xbias[l].at(b))
                    for k in range(NT):
                        u = use["y", l, k]
                        if l == 1:
                            dve.wait_ge(filled[u.bank], u.filled_at)
                            v.scalar_tensor_tensor(out=X[1][:, k, :], in0=bank(u.bank), scalar=1.0 / WS, in1=X[1][:, k, :],
                                                   op0=ALU.mult, op1=ALU.add).then_inc(read[u.bank], 1)
                            continue
                        if k == 0:
                            dve.wait_ge(qf_biased.sem, qf_biased.at(b))
                        dve.wait_ge(filled[u.bank], u.filled_at)
                        v.scalar_tensor_tensor(out=yf[k], in0=bank(u.bank), scalar=1.0 / WS, in1=qf0[:, k, :],
                                               op0=ALU.mult, op1=ALU.add).then_inc(read[u.bank], 1)
                        dve.wait_ge(read[u.bank], u.read_at)
                        ln_stats("E", yf[k], k, stats_E.sem)
                    if l == 0:
                        for k in range(NT):
                            dve.wait_ge(rstd_E.sem, rstd_E.at(b, k + 1))
                            chain(v.scalar_tensor_tensor(out=yf[k], in0=yf[k], scalar=mv["E"][:, k, 0:1],
                                                         in1=rows["L0_xattn_ln_gamma"], op0=ALU.subtract, op1=ALU.mult))
                            v.scalar_tensor_tensor(out=xp[:, k, :], in0=yf[k], scalar=rs["E"][:, k:k + 1], in1=X[0][:, k, :],
                                                   op0=ALU.mult, op1=ALU.add).then_inc(xp_ready.sem, 1)
                            dve.wait_ge(xp_ready.sem, xp_ready.at(b, k + 1))
                            ln_stats("F", xp[:, k, :], k, stats_F.sem)
                if 0 in streams:
                    b = i
                    for k in range(NT):
                        dve.wait_ge(rstd_F.sem, rstd_F.at(b, k + 1))
                        normalise("F", xn[0][:, k, :], xp[:, k, :], k, xnF_ready.sem)
                    for k in range(NT):
                        lo(use["xf", k], cols(xT[0], 1, k), cols(xT[0], 0, k), xF_hi.sem, xF_hi.at(b, k + 1))
                    for k in range(NT):
                        u = use["had", k]
                        dve.wait_ge(filled[u.bank], u.filled_at)
                        chain(v.tensor_reduce(am[:, k:k + 1], bank(u.bank), AX_X, ALU.max, apply_absolute_value=True))
                        chain(v.tensor_scalar(am[:, k:k + 1], am[:, k:k + 1], HAD, 1e-5, ALU.mult, ALU.max))
                        v.tensor_scalar(qsc[:, k:k + 1], am[:, k:k + 1], 1.0 / 7.0, None, ALU.mult).then_inc(absmax.sem, 1)
                    for k in range(NT):
                        u = use["had", k]
                        dve.wait_ge(read[u.bank], u.read_at)
                        v.tensor_scalar(nq[:, k, :], tq[k], MAGIC, 7.0, ALU.subtract, ALU.min).then_inc(nq_ready.sem, 1)
                    for k in range(NT):
                        u = use["f0", k]
                        dve.wait_ge(filled[u.bank], u.filled_at)
                        v.scalar_tensor_tensor(out=tq[k], in0=bank(u.bank), scalar=qsc[:, k:k + 1], in1=wsc_row,
                                               op0=ALU.mult, op1=ALU.mult).then_inc(read[u.bank], 1)

            def attn_out(l, b, g, u):
                dve.wait_ge(av_done[l].sem, av_done[l].at(b, (g + 1) * HG))
                o = bank(u.bank)[:, 0:NT * HG * OW].rearrange("p (t h d) -> p t h d", t=NT, h=HG)
                chain(v.reciprocal(rden[l], o[:, :, :, HD]))
                dst = xn[l].rearrange("p t (h d) -> p t h d", h=H)[:, :, g * HG:(g + 1) * HG, :]
                for k in range(NT):
                    ins = v.tensor_tensor(dst[:, k], o[:, k, :, 0:HD], rden[l][:, k, :].unsqueeze(2).to_broadcast([P, HG, HD]), ALU.mult)
                    if k == NT - 1:
                        ins.then_inc(read[u.bank], 1)

            steps(dve, step, chain)

            for w in range(2):
                dve.wait_ge(wb_loaded, 48 if w == 0 else 64)
                if w:
                    dve.wait_ge(wtr_filled, 8)
                chain(v.tensor_reduce(wab, wst.rearrange("p (c n) -> p c n", c=FC), AX_X, ALU.add, apply_absolute_value=True))
                v.tensor_reduce(wsum[:, w:w + 1], wab, AX_X, ALU.add).then_inc(wb_part, 1)
                dve.wait_ge(wb_sum, w + 1)
                chain(v.tensor_scalar(wthr[:, 0:1], bank(5)[:, 0:1], 1.0 / (D * FF), 1e-8, ALU.mult, ALU.max))
                chain(v.tensor_scalar(wthr[:, 1:2], wthr[:, 0:1], 0.5, None, ALU.mult))
                chain(v.tensor_scalar(wthr[:, 2:3], wthr[:, 0:1], -0.5, None, ALU.mult))
                chain(v.tensor_scalar(wgt, wst, wthr[:, 2:3], None, ALU.is_lt))
                v.scalar_tensor_tensor(out=wtern, in0=wst, scalar=wthr[:, 1:2], in1=wgt, op0=ALU.is_gt,
                                       op1=ALU.subtract).then_inc(wb_tern, 1)
                dve.wait_ge(wb_tern, w + 1)

            def prep_b(s, slot, r):
                dve.wait_ge(xb_loaded[slot], r * (16 * GB) + 16 * GB)
                for k in range(BT):
                    ln_stats("B", Xb[slot][:, k, :], k, statsB)
                dve.wait_ge(rstdB, s + 1)
                dve.wait_ge(statsB, s * BT + BT)
                for k in range(BT):
                    normalise("B", xnb[:, k, :], Xb[slot][:, k, :], k, xnb_ready)

            def split_b(s):
                for k in range(BT):
                    dve.wait_ge(xTb_hi, s * BT + k + 1)
                    v.tensor_tensor(xTb[:, 1, :, k * P:(k + 1) * P], bank(6 + k % 2).rearrange("p (c n) -> p c n", c=DC),
                                    xTb[:, 0, :, k * P:(k + 1) * P], ALU.subtract).then_inc(xTb_read, 1)

            def step_b(s, slot, r, has_next):
                for f in range(FC):
                    dve.wait_ge(gelu_done, s * FC + f + 1)
                    later(dve, g_used, s * FC + f + 1 - NG)
                    v.tensor_copy(gh[:, f % NG, :], gf[f % 2]).then_inc(g_hi, 1)
                    if f % 2:
                        dve.wait_ge(g_hi, s * FC + f + 1)
                        v.tensor_tensor(gl[:, f % NG, :], gf[f % 2], gh[:, f % NG, :], ALU.subtract).then_inc(g_lo[1], 1)
                    if f == PREP and has_next:
                        prep_b(s + 1, 1 - slot, r + slot)
                if has_next:
                    split_b(s + 1)
                dve.wait_ge(xb_biased, s + 1)
                dve.wait_ge(g_used, s * FC + FC)
                for k in range(BT):
                    v.tensor_tensor(Xb[slot][:, k, :], bank(k), Xb[slot][:, k, :], ALU.add).then_inc(yb_ready, 1)

            prep_b(0, 0, 0)
            split_b(0)
            steps_b(step_b, dve, chain)

        @block.tensor
        def _(pe):
            te = nc.tensor
            pe.wait_ge(const_ready, CONSTS)
            pe.wait_ge(setup_dve, 3)
            for c in range(DC):
                mm = te.matmul(bank(0)[:, c * P:(c + 1) * P], wsum_rows[:, c:c + 1].to_broadcast([P, P]), ident,
                               start=True, stop=True)
            mm.then_inc(setup_pe, 1)
            for c in range(DC):
                for o in range(DC):
                    mm = te.transpose(bank(c + 1).bitcast(F16)[:, o * P:(o + 1) * P], tr0[:, o, c * P:(c + 1) * P], identh)
                mm.then_inc(setup_pe, 1)
            pe.wait_ge(w_split, len(W))
            pe.wait_ge(setup_act, DC + 1)

            def open_bank(u):
                if not (isinstance(u.free_at, int) and u.free_at == 0):
                    pe.wait_ge(read[u.bank], u.free_at)

            def product(out, lhs, w, k, chunks):
                for c in range(chunks):
                    x_hi, x_lo = (lhs[:, s, c, k * P:(k + 1) * P] for s in range(2))
                    te.matmul(out, x_hi, w[:, 0, c, :], start=(c == 0), stop=False)
                    te.matmul(out, x_hi, w[:, 1, c, :], start=False, stop=False)
                    mm = te.matmul(out, x_lo, w[:, 0, c, :], start=False, stop=(c == chunks - 1))
                return mm

            def turn(u, src, chunks):
                open_bank(u)
                for c in range(chunks):
                    mm = te.transpose(bank(u.bank)[:, c * P:(c + 1) * P], src[:, c * P:(c + 1) * P], ident)
                mm.then_inc(filled[u.bank], 1)

            def step(streams, i, use):
                bs = {0: i, 1: i - 1}
                for l in streams:
                    b = bs[l]
                    for k in range(NT):
                        pe.wait_ge(xn_ready[l].sem, xn_ready[l].at(b, k + 1))
                        turn(use["x", l, k], xn[l][:, k, :], DC)
                    if l == 0:
                        pe.wait_ge(ctx_loaded.sem, ctx_loaded.at(b))
                        for k in range(NT):
                            turn(use["c", k], CT[:, k, :], CC)
                for l in streams:
                    b = bs[l]
                    if l == 1:
                        pe.wait_ge(ctxT_copied.sem, ctxT_copied.at(b))
                    for k in range(NT):
                        u = use["x", l, k]
                        pe.wait_ge(read[u.bank], u.read_at)
                        if l == 0:
                            u = use["c", k]
                            pe.wait_ge(read[u.bank], u.read_at)
                        for j, m in enumerate("qkv"):
                            u = use["qkv", l, k, j]
                            open_bank(u)
                            src, n = (xT[l], DC) if m == "q" else (cT[l], CC)
                            product(bank(u.bank), src, wsplit[l, m], k, n).then_inc(filled[u.bank], 1)
                for l in streams:
                    b = bs[l]
                    for k in range(NT):
                        for j in range(2):
                            pe.wait_ge(qk_hi[l].sem, qk_hi[l].at(b, 2 * k + j + 1))
                            pe.wait_ge(qk_lo[l].sem, qk_lo[l].at(b, 2 * k + j + 1))
                            for g in range(2):
                                u = use["st", l, k, j, g]
                                open_bank(u)
                                out = bank(u.bank).bitcast(F16)
                                for h in range(8):
                                    src = qks[l][:, j, k, g * 8 + h].rearrange("p s d -> p (s d)")
                                    mm = te.transpose(out[0:QW, h * P:(h + 1) * P], src, identh)
                                mm.then_inc(filled[u.bank], 1)
                if 1 in streams:
                    all_read(pe, [use["st", 1, k, j, g] for k in range(NT) for j in range(2) for g in range(2)])
                    for h in range(H):
                        u = use["mx", h]
                        open_bank(u)
                        for k in range(NT):
                            mm = te.matmul(bank(u.bank)[:, k * S:(k + 1) * S], qkT[1][0:QW, 0, h, k * P:(k + 1) * P],
                                           qkT[1][0:QW, 1, h, :], start=True, stop=True)
                        mm.then_inc(filled[u.bank], 1)
                if 0 in streams:
                    all_read(pe, [use["st", 0, k, j, g] for k in range(NT) for j in range(2) for g in range(2)])
                for n in range(H + 3):
                    if 1 in streams and 1 <= n <= H:
                        h = n - 1
                        if h == 0:
                            pe.wait_ge(shift_ready.sem, shift_ready.at(bs[1]))
                        pe.wait_ge(clipped.sem, clipped.at(bs[1], h + 1))
                        u = use["s", 1, h]
                        out = bank(u.bank).rearrange("p (k t n) -> p k t n", k=NT, t=NT)
                        for k in range(NT):
                            mm = te.matmul(out[:, :, k, :], mneg[:, k, h:h + 1].to_broadcast([P, P]),
                                           identh.unsqueeze(1).to_broadcast([P, NT, P]), start=False, stop=True,
                                           skip_group_check=True)
                        mm.then_inc(shifted.sem, 1)
                    for l in (0, 1):
                        if l in streams and n < H:
                            u = use["s", l, n]
                            open_bank(u)
                            for k in range(NT):
                                mm = te.matmul(bank(u.bank)[:, k * S:(k + 1) * S], qkT[l][0:QW, 1, n, k * P:(k + 1) * P],
                                               qkT[l][0:QW, 0, n, :], start=(k == 0), stop=True,
                                               skip_group_check=True)
                            mm.then_inc(filled[u.bank], 1)
                    for l in (0, 1):
                        h = n - 2 - l
                        if l in streams and 0 <= h < H:
                            attend(l, bs[l], h, use["o", l, h // HG])
                for l in streams:
                    all_read(pe, [use["o", l, g] for g in range(H // HG)])
                    for k in range(NT):
                        turn(use["ot", l, k], xn[l][:, k, :], DC)
                for l in streams:
                    for k in range(NT):
                        u = use["ot", l, k]
                        pe.wait_ge(read[u.bank], u.read_at)
                        u = use["y", l, k]
                        open_bank(u)
                        product(bank(u.bank), xT[l], wsplit[l, "o"], k, DC).then_inc(filled[u.bank], 1)
                if 0 in streams:
                    b = i
                    for k in range(NT):
                        pe.wait_ge(xnF_ready.sem, xnF_ready.at(b, k + 1))
                        turn(use["xf", k], xn[0][:, k, :], DC)
                    for k in range(NT):
                        u = use["xf", k]
                        pe.wait_ge(read[u.bank], u.read_at)
                        u = use["had", k]
                        open_bank(u)
                        hs = had[:, 0:4 * P]
                        rows4 = [hs[:, 0:P].unsqueeze(1).to_broadcast([P, 4, P]),
                                 hs[:, 0:2 * P].unsqueeze(1).to_broadcast([P, 2, 2 * P]),
                                 hs[:, 0:2 * P].rearrange("p (a n) -> p a n", a=2).unsqueeze(2).to_broadcast([P, 2, 2, P]),
                                 hs]
                        for c in range(DC):
                            for s in range(2):
                                mm = te.matmul(bank(u.bank), xT[0][:, s, c, k * P:(k + 1) * P], rows4[c],
                                               start=(c + s == 0), stop=(c + s == DC))
                        mm.then_inc(filled[u.bank], 1)
                    for k in range(NT):
                        pe.wait_ge(nq_ready.sem, nq_ready.at(b, k + 1))
                        u = use["nt", k]
                        open_bank(u)
                        for c in range(DC):
                            mm = te.transpose(bank(u.bank).bitcast(F16)[:, c * P:(c + 1) * P], nq[:, k, c * P:(c + 1) * P], identh)
                        mm.then_inc(filled[u.bank], 1)
                    for k in range(NT):
                        u = use["nt", k]
                        pe.wait_ge(read[u.bank], u.read_at)
                        u = use["f0", k]
                        open_bank(u)
                        for c in range(DC):
                            mm = te.matmul(bank(u.bank), nT[:, c, k * P:(k + 1) * P], tern0[:, c, :],
                                           start=(c == 0), stop=(c == DC - 1))
                        mm.then_inc(filled[u.bank], 1)

            def attend(l, b, h, u):
                if h % HG == 0:
                    open_bank(u)
                if h == 0:
                    pe.wait_ge(v_lo[l].sem, v_lo[l].at(b))
                if lo_on_dve[l][h]:
                    pe.wait_ge(p_lo_dve[l].sem, p_lo_dve[l].at(b, sum(lo_on_dve[l][:h + 1])))
                else:
                    pe.wait_ge(p_lo_pool[l].sem, p_lo_pool[l].at(b, h + 1 - sum(lo_on_dve[l][:h + 1])))
                for q in range(NT):
                    at = (q * HG + h % HG) * OW
                    out = bank(u.bank)[:, at:at + OW]
                    for k in range(NT):
                        p_hi_t = ph[l][:, h % NP, k * S + q * P:k * S + (q + 1) * P]
                        p_lo_t = pl[l][:, h % NP, k * S + q * P:k * S + (q + 1) * P]
                        te.matmul(out, p_hi_t, vs[l][:, k, h, 0:OW], start=(k == 0), stop=False)
                        te.matmul(out[:, 0:HD], p_hi_t, vs[l][:, k, h, HD + 2:VP], start=False, stop=False)
                        mm = te.matmul(out, p_lo_t, vs[l][:, k, h, 0:OW], start=False, stop=(k == NT - 1))
                mm.then_inc(av_done[l].sem, 1)

            steps(pe, step)

            for w in range(2):
                pe.wait_ge(wb_part, w + 1)
                te.matmul(bank(5)[:, 0:1], one_col.to_broadcast([P, P]), wsum[:, w:w + 1], start=True, stop=True).then_inc(wb_sum, 1)
                pe.wait_ge(wb_tern, w + 1)
                src = wtern.rearrange("p (c n) -> p c n", c=FC if w == 0 else DC)
                for g in range(8):
                    if w * 8 + g >= 4:
                        pe.wait_ge(wtr_read, w * 8 + g - 3)
                    for n in range(8):
                        out = bank(g % 4).bitcast(F16)[:, n * P:(n + 1) * P]
                        if w == 0:
                            s = src[:, (g // DC) * 8 + n, (g % DC) * P:(g % DC + 1) * P]
                        else:
                            f = (g // 4) * 8 + n
                            s = src[:, g % 4, f * P:(f + 1) * P]
                        mm = te.transpose(out, s, identh)
                    mm.then_inc(wtr_filled, 1)
            pe.wait_ge(wtr_read, 16)

            def turn_b(s):
                for k in range(BT):
                    pe.wait_ge(xnb_ready, s * BT + k + 1)
                    later(pe, xTb_read, s * BT + k - 1)
                    for c in range(DC):
                        mm = te.transpose(bank(6 + k % 2)[:, c * P:(c + 1) * P], xnb[:, k, c * P:(c + 1) * P], ident)
                    mm.then_inc(xTb_filled, 1)

            def up(s, f):
                later(pe, gelu_done, s * FC + f - 1)
                for c in range(DC):
                    for part in range(2):
                        mm = te.matmul(bank(4 + f % 2), w1T[:, c, f * P:(f + 1) * P], xTb[:, part, c, :],
                                       start=(c + part == 0), stop=(c + part == DC))
                mm.then_inc(h_filled, 1)

            def down(s, f):
                if f == 0:
                    later(pe, yb_ready, s * BT)
                g_lo_wait(pe, s, f)
                for k in range(BT):
                    for n, src in enumerate((gh, gl)):
                        mm = te.matmul(bank(k), src[:, f % NG, k * P:(k + 1) * P], w2T[:, f, :],
                                       start=(f + n == 0), stop=(f + n == FC))
                mm.then_inc(g_used, 1)

            def step_b(s, slot, r, has_next):
                pe.wait_ge(xTb_read, s * BT + BT)
                up(s, 0)
                up(s, 1)
                for f in range(FC):
                    if f == FC - 2 and has_next:
                        turn_b(s + 1)
                    down(s, f)
                    if f + 2 < FC:
                        up(s, f + 2)

            turn_b(0)
            steps_b(step_b, pe)


_ROWS = ["L0_xattn_bq", "L0_xattn_bk", "L0_xattn_bv", "L0_xattn_bo", "L0_xattn_ln_gamma", "L0_xattn_ln_beta",
         "L1_xattn_bq", "L1_xattn_bk", "L1_xattn_bv", "L1_xattn_bo"]
_INS = ["x", "ctx_768", "L0_xattn_Wq", "L0_xattn_Wk", "L0_xattn_Wv", "L0_xattn_Wo", "L0_ffn_weight",
        "L1_xattn_Wq", "L1_xattn_Wk", "L1_xattn_Wv", "L1_xattn_Wo", "L1_ffn_W1", "L1_ffn_b1", "L1_ffn_W2",
        "L1_ffn_b2"] + _ROWS


def hadamard_signs():
    h = np.array([[1.0]])
    while h.shape[0] < P:
        h = np.block([[h, h], [h, -h]])
    return np.concatenate([h, -h, -h, h], axis=1).astype(np.float16)


def kernel(**inputs):
    from concourse import bacc
    from concourse.bass_utils import run_bass_kernel_spmd

    nc = bacc.Bacc("TRN2", target_bir_lowering=False, num_devices=1)
    arrays, t = {}, {}
    for name in _INS:
        arrays[f"in_{name}"] = np.ascontiguousarray(inputs[name])
    arrays["in_signs"] = hadamard_signs()
    for name, a in arrays.items():
        t[name[3:]] = nc.dram_tensor(name, a.shape, mybir.dt.from_np(a.dtype), kind="ExternalInput").ap()
    t["out"] = nc.dram_tensor("out_0", (B, S, D), F32, kind="ExternalOutput").ap()
    xattn_ffn(nc, t)
    r = run_bass_kernel_spmd(nc, [arrays], core_ids=[0])
    return r.results[0]["out_0"]
```

```python
from contextlib import ExitStack

import numpy as np

import concourse.bass as bass
from concourse import mybir

P = 128
F32 = mybir.dt.float32
F16 = mybir.dt.float16
ACT = mybir.ActivationFunctionType
ALU = mybir.AluOpType
AX_X = mybir.AxisListType.X

B, S, D, CD = 16, 256, 512, 384
H, HD = 16, 32
FF = 2048
NT = S // P
DC, CC, FC = D // P, CD // P, FF // P
EPS = 1e-5
SCALE = HD ** -0.5
CLAMP = 1e4
MAGIC = 1.5 * 2.0 ** 23
WS = 64.0
QS = 32.0
HAD = float(np.float32(1.0 / np.sqrt(D)))
QW = 3 * HD
VP = 66
OW = 33
HG = 4
WC = 4
GB = 2
BT = GB * NT
STATS_AT, NORM_AT, TURN_AT = 3, 7, 9


class Signal:

    def __init__(self, sem, per_batch):
        self.sem, self.per_batch = sem, per_batch

    def at(self, b, k=None):
        return b * self.per_batch + (self.per_batch if k is None else k)


class Chain:

    def __init__(self, eng, sem):
        self.eng, self.sem, self.n, self.offset = eng, sem, 0, 0

    def __call__(self, ins):
        ins.then_inc(self.sem, 1)
        self.n += 1
        self.eng.wait_ge(self.sem, self.offset + self.n)


RUNS = (0, 2, 1, 1, 1, 1, 1, 2, 3, 4, 4, 1, 1, 1, 1, 1, 1, 1, 2, 1, 2, 1, 4, 1, 6, 1, 2, 1, 1, 2, 2, 6, 1, 1,
        3, 2, 2, 1, 2, 3, 2, 1, 3, 2, 1, 1, 5, 1, 2, 2, 1, 2, 1, 3, 1, 2, 2, 1, 1, 2, 1, 1, 2, 5, 4, 11, 2, 7,
        6, 1, 1, 1, 3, 2, 1, 1, 5, 1, 1, 1, 1, 1, 1, 1, 6)
EARLY_MAXIMA = 8
UPPER_ON_ACT = (False, False)
AV_LAG = (3, 4)


def fills(task):
    kind, l, *at = task
    simple = {"turn_x": ("x", "T"), "turn_ctx": ("c", "T"), "stack": ("st", "T"), "maxima": ("mx", "J"),
              "turn_out": ("ot", "S"), "out_project": ("y", "O"), "turn_ffn": ("xf", "S"), "hadamard": ("had", "O"),
              "turn_levels": ("nt", "S"), "ffn0": ("f0", "O")}
    out = []
    if kind in simple:
        name, pool = simple[kind]
        out.append(((name, l, *at), pool))
    elif kind == "project" and at[2] == 0:
        out.append((("qkv", l, *at[:2]), "J"))
    elif kind == "head":
        if at[0] < H:
            out.append((("s", l, at[0]), "S"))
        h = at[0] - AV_LAG[l]
        if 0 <= h < H and h % HG == 0:
            out.append((("o", l, h // HG), "O"))
    return out


def frees(task):
    kind, l, *at = task
    simple = {"split_x": "x", "split_ctx": "c", "stack": "st", "maxima": "mx", "split_out": "ot", "out": "y",
              "split_ffn": "xf", "round": "had", "turn_levels": "nt", "ffn0_out": "f0", "bias": "qkv"}
    if kind in simple:
        return [(simple[kind], l, *at)]
    if kind == "head":
        return [("s", l, at[0] - l), ("o", l, (at[0] - AV_LAG[l] - HG) // HG)]
    return []


def merged(streams, runs):
    out, gone = [], set()
    free, bank_of = {pool: list(banks) for pool, banks in POOLS.items()}, {}
    for task in [streams[n % 2].pop(0) for n, run in enumerate(runs) for _ in range(run)]:
        out.append(task)
        used = frees(task)
        for name, pool in fills(task):
            if not free[pool]:
                free[pool] = [bank_of[x] for x in used if bank_of.get(x) in POOLS[pool] and x not in gone][:1]
                gone |= {x for x in used if bank_of.get(x) == free[pool][0]}
            bank_of[name] = free[pool].pop(0)
        for name in frees(task):
            if name in bank_of and name not in gone:
                gone.add(name)
                free[[p for p in POOLS if bank_of[name] in POOLS[p]][0]].append(bank_of[name])
    return out, bank_of


def front(l):
    out = [("stats", l), ("normalise", l)]
    out += [("turn_x", l, k) for k in range(NT)] + [("split_x", l, k) for k in range(NT)]
    if l == 0:
        out += [("turn_ctx", 0, k) for k in range(NT)] + [("split_ctx", 0, k) for k in range(NT)]
    stacks = [[("stack", l, k, j, g) for j in range(2) for g in range(2)] for k in range(NT)]
    for k in range(NT):
        late = []
        for j in range(3):
            out += [("project", l, k, j, 0)] + late + [("project", l, k, j, 1)]
            late = [("bias", l, k, j)]
        out += late + [("norm", l, k), ("upper_qk", l, k), ("lower_qk", l, k)]
    for k in range(NT):
        out += stacks[k]
    if l == 1:
        out += [("maxima", 1, h) for h in range(EARLY_MAXIMA)]
    return out


def heads_of(l):
    first = [("maxima", 1, h) for h in range(EARLY_MAXIMA, H)] + [("shifts", 1)] if l == 1 else []
    return first + [("head", l, n) for n in range(H + AV_LAG[l] + 1)]


def back(l):
    ks = range(NT)
    out = [(kind, l, k) for kind in ("turn_out", "split_out", "out_project", "out") for k in ks]
    if l == 0:
        out += [(kind, 0, k) for kind in ("post_norm", "normalise_ffn", "turn_ffn", "split_ffn", "hadamard", "absmax",
                                          "round", "levels", "turn_levels", "ffn0", "ffn0_out") for k in ks]
        out += [("store_x1", 0)]
    return out


POOLS = {"T": (0, 1), "J": (2, 3), "S": (5, 6), "O": (4, 7)}
TASKS, BANK_OF = merged([front(0) + heads_of(0) + back(0), heads_of(1) + back(1) + front(1)], RUNS)
BACK = set(heads_of(1) + back(1))


def task_order(active):
    parts = [("0" if task[1] == 0 else "1b" if task in BACK else "1f", task) for task in TASKS]
    return [(part, task) for part, task in parts if part in active]


def pe_fills(active):
    return [name for _, task in task_order(active) for name, _ in fills(task)]


class Use:

    def __init__(self, bank, filled_at, free_at, read_at):
        self.bank, self.filled_at, self.free_at, self.read_at = bank, filled_at, free_at, read_at


def plan(active, base, offset):
    count = [[0] * 8, [0] * 8]
    uses = {}
    for name in pe_fills(active):
        n = BANK_OF[name]
        count[0][n] += name[0] != "o"
        count[1][n] += 1
        filled, read = (base[k][n] + count[k][n] for k in range(2))
        if offset is None:
            uses[name] = Use(n, filled, read - 1, read)
        else:
            uses[name] = Use(n, offset[0][n] + filled, offset[1][n] + (read - 1), offset[1][n] + read)
    return uses, count


ALL = ("0", "1f", "1b")


def plus(base, counts, times=1):
    return [[a + times * n for a, n in zip(x, y)] for x, y in zip(base, counts)]


def steps(eng, emit, chain=None):
    base = [[0] * 8] * 2

    def alone(active, i):
        uses, counts = plan(active, base, None)
        emit(active, i, uses)
        return plus(base, counts)

    base = alone(("0",), 0)
    base = alone(("0", "1f"), 1)
    before = chain.n if chain else 0
    base = alone(ALL, 2)
    per = chain.n - before if chain else 0
    both = plan(ALL, base, None)[1]
    with eng.Fori(3, B) as i:
        if chain:
            chain.offset = (i - 3) * per
        since = {n: (i - 3) * n for n in sorted({n for x in both for n in x})}
        emit(ALL, i, plan(ALL, base, [[since[n] for n in x] for x in both])[0])
    if chain:
        chain.offset = 0
        chain.n += per * (B - 4)
    base = plus(base, both, B - 3)
    base = alone(("1f", "1b"), B)
    alone(("1b",), B + 1)


def xattn_ffn(nc, t):
    with ExitStack() as ctx:
        def sem(name):
            return ctx.enter_context(nc.semaphore(name))

        def dram(name, shape, dt=F32):
            return nc.dram_tensor(name, shape, dt, kind="Internal").ap()

        psum = ctx.enter_context(nc.psum_tensor("psum", [P, 8, 512], F32))
        words = 192 * 1024 // 4
        arena = ctx.enter_context(nc.sbuf_tensor("arena", [P, words], F32))
        top = [0]

        def take(n):
            top[0] += n
            assert top[0] <= words, top[0]
            return arena[:, top[0] - n:top[0]]

        def bank(n):
            return psum[:, n, :]

        ident = take(P)
        identh = take(P // 2).bitcast(F16)
        had = take(2 * P).bitcast(F16)
        small = take(320)
        row_names = ["L0_xattn_bq", "L0_xattn_bk", "L0_xattn_bv", "L0_xattn_bo", "L0_xattn_ln_gamma",
                     "L0_xattn_ln_beta", "L1_xattn_bq", "L1_xattn_bk", "L1_xattn_bv", "L1_xattn_bo"]
        rows = {n: take(D) for n in row_names}
        wsc_row = take(D)
        b2_row = rows["L0_xattn_bq"]
        at_phase_b = top[0]
        tern0 = take(DC * D // 2).bitcast(F16).rearrange("p (c n) -> p c n", c=DC)
        wsplit = {}
        for l in range(2):
            for m, c in (("q", DC), ("k", CC), ("v", CC), ("o", DC)):
                wsplit[l, m] = take(c * D).bitcast(F16).rearrange("p (s c n) -> p s c n", s=2, c=c)

        def tiles(ap, n=NT):
            return ap.rearrange("p (t n) -> p t n", t=n)

        X = [tiles(take(NT * D)) for _ in range(2)]
        xn = [tiles(take(NT * D)) for _ in range(2)]
        xT_raw = [take(DC * S) for _ in range(2)]
        xT = [a.bitcast(F16).rearrange("p (s c n) -> p s c n", s=2, c=DC) for a in xT_raw]
        cT_raw = [take(CC * S) for _ in range(2)]
        cT = [a.bitcast(F16).rearrange("p (s c n) -> p s c n", s=2, c=CC) for a in cT_raw]
        qf0 = tiles(take(NT * D))
        kv0 = take(4 * D)
        qk_raw = [take(2 * NT * H * QW // 2) for _ in range(2)]
        qks = [a.bitcast(F16).rearrange("p (j t h s d) -> p j t h s d", j=2, t=NT, h=H, s=3) for a in qk_raw]

        def qk_hi_of(l, j, k):
            return qks[l][:, j, k, :, 0:3:2 - j, :] if j == 0 else qks[l][:, j, k, :, 0:2, :]

        def qk_one_hi_of(l, j, k):
            return qks[l][:, j, k, :, 0, :]

        def qk_lo_of(l, j, k):
            return qks[l][:, j, k, :, 1 + j, :]

        vs = [take(NT * H * VP // 2).bitcast(F16).rearrange("p (t h d) -> p t h d", t=NT, h=H) for _ in range(2)]
        qkT_raw = [take(2 * H * S // 2) for _ in range(2)]
        qkT = [a.bitcast(F16).rearrange("p (j h n) -> p j h n", j=2, h=H) for a in qkT_raw]
        kv1 = qkT_raw[1][:, H * S - 3 * D:H * S]
        kf0 = [kv0[:, 0:D], kv0[:, D:2 * D]]
        vf0 = [kv0[:, 2 * D:3 * D], kv0[:, 3 * D:4 * D]]
        CT = tiles(kv0[:, 2 * D:2 * D + NT * CD])
        tq = kf0
        yf = vf0
        pf = [vf0, [xT_raw[1][:, 0:D], xT_raw[1][:, D:2 * D]]]
        xp = qf0
        NP = 3
        ph = [qk_raw[l][:, 0:NP * D // 2].bitcast(F16).rearrange("p (r n) -> p r n", r=NP) for l in range(2)]
        pl = [qk_raw[l][:, NP * D // 2:NP * D].bitcast(F16).rearrange("p (r n) -> p r n", r=NP) for l in range(2)]
        nq = tiles(qk_raw[0][:, 0:NT * D // 2].bitcast(F16))
        nT = qk_raw[0][:, NT * D // 2:NT * D].bitcast(F16).rearrange("p (c n) -> p c n", c=DC)

        sm = [0]

        def tiny(n):
            sm[0] += n
            return small[:, sm[0] - n:sm[0]]

        magic = tiny(1)
        half4 = tiny(4)
        eps4, qs4, had4 = tiny(4), tiny(4), tiny(4)
        one4 = tiny(4)
        st = tiny(6 * 4)
        mv = {k: tiny(2 * 4).rearrange("p (t k) -> p t k", k=2) for k in ("A0", "A1", "E", "F", "B")}
        rs = {k: tiny(4) for k in ("A0", "A1", "E", "F", "B")}
        tmp = {k: tiny(4) for k in ("A0", "A1", "E", "F", "B", "N", "Q")}
        ssq = tiny(4)
        rn = tiny(4)
        am = tiny(NT)
        qsc = tiny(NT)
        qrs = tiny(NT)
        mx = tiny(NT * H).rearrange("p (t h) -> p t h", t=NT)
        mneg = tiny(NT * H // 2).bitcast(F16).rearrange("p (t h) -> p t h", t=NT)
        rden = [tiny(NT * HG).rearrange("p (t h) -> p t h", t=NT) for _ in range(2)]
        wab = tiny(2 * WC)
        wsum = tiny(2)
        wthr = tiny(8)
        wsum_rows = tiny(DC)
        one_col = tiny(1)

        b1c = tiny(FC)
        top[0] = at_phase_b
        w1T = take(DC * FF // 2).bitcast(F16).rearrange("p (c f) -> p c f", c=DC)
        w2T = take(FC * D // 2).bitcast(F16).rearrange("p (c n) -> p c n", c=FC)
        Xb = [tiles(take(BT * D), BT) for _ in range(2)]
        xnb = tiles(kv0, BT)
        xTb = [take(DC * BT * P).bitcast(F16).rearrange("p (s c n) -> p s c n", s=2, c=DC)]
        gf = [take(BT * P) for _ in range(2)]
        NG = 4
        gh = take(NG * BT * P // 2).bitcast(F16).rearrange("p (r n) -> p r n", r=NG)
        xTb.append(take(DC * BT * P).bitcast(F16).rearrange("p (s c n) -> p s c n", s=2, c=DC))
        gl = take(NG * BT * P // 2).bitcast(F16).rearrange("p (r n) -> p r n", r=NG)

        xd = t["x"].rearrange("b (t p) d -> b p t d", p=P)
        cd = t["ctx_768"].rearrange("b (t p) d -> b p t d", p=P)
        od = t["out"].rearrange("b (t p) d -> b p t d", p=P)
        x1d = dram("x1_scratch", [B, P, NT * D]).rearrange("b p (t d) -> b p t d", t=NT)
        x2d = dram("x2_scratch", [B, P, NT * D]).rearrange("b p (t d) -> b p t d", t=NT)

        def batch(d, b):
            return d[b] if isinstance(b, int) else d[bass.ds(b, 1)].rearrange("a p t d -> p (a t) d")

        filled = [sem(f"bank{n}_filled") for n in range(8)]
        read = [sem(f"bank{n}_read") for n in range(8)]
        CONSTS = 13
        const_ready = sem("const_ready")
        consts_loaded = sem("consts_loaded")
        w_loaded = [sem(f"w_loaded{n}") for n in range(2)]
        w_split = sem("w_split")
        w_hi = sem("w_hi")
        setup_pe = sem("setup_pe")
        setup_dve = sem("setup_dve")
        setup_act = sem("setup_act")
        dve_step, pool_step = sem("dve_step"), sem("pool_step")

        def signals(name, *per_batch):
            return [Signal(sem(f"{name}_{l}"), k) for l, k in enumerate(per_batch)]

        x_loaded = signals("x_loaded", 16, 16)
        ctx_loaded = Signal(sem("ctx_loaded"), 16)
        ctxT_copied = Signal(sem("ctxT_copied"), 16)
        x1_stored = Signal(sem("x1_stored"), 16)
        x2_stored = Signal(sem("x2_stored"), 16)
        stats_A = signals("statsA", 2, 2)
        rstd_A = signals("rstdA", 1, 1)
        xn_ready = signals("xn_ready", 2, 2)
        xT_hi = signals("xT_hi", NT, NT)
        ctxT_hi = Signal(sem("ctxT_hi"), NT)
        oT_hi = signals("oT_hi", NT, NT)
        xbias = signals("xbias", 1, 1)
        squares = Signal(sem("squares"), 4)
        guarded = Signal(sem("guarded"), NT)
        norms = Signal(sem("norms"), NT)
        qk_hi = signals("qk_hi", 4, 4)
        qk_lo = signals("qk_lo", 4, 4)
        v_hi = signals("v_hi", NT, NT)
        v_lo = signals("v_lo", NT, NT)
        shift_ready = Signal(sem("shift_ready"), 1)
        clipped = Signal(sem("clipped"), H)
        shifted = Signal(sem("shifted"), H)
        p_hi = signals("p_hi", H, H)
        p_lo = signals("p_lo", H, H)
        av_done = signals("av_done", H, H)
        qf_biased = Signal(sem("qf_biased"), 1)
        stats_E = Signal(sem("statsE"), 2)
        rstd_E = Signal(sem("rstdE"), 2)
        xp_ready = Signal(sem("xp_ready"), 2)
        stats_F = Signal(sem("statsF"), 2)
        rstd_F = Signal(sem("rstdF"), 2)
        xnF_ready = Signal(sem("xnF_ready"), 2)
        xF_hi = Signal(sem("xF_hi"), 2)
        absmax = Signal(sem("absmax"), 2)
        qscale = Signal(sem("qscale"), 2)
        nq_ready = Signal(sem("nq_ready"), 2)
        x1_ready = Signal(sem("x1_ready"), 2)

        biasb_loaded = sem("biasb_loaded")
        wb_loaded = [sem(f"wb_loaded{n}") for n in range(2)]
        wb_used, wb_sum, wb_part = sem("wb_used"), sem("wb_sum"), sem("wb_part")
        wtr_filled, wtr_read = sem("wtr_filled"), sem("wtr_read")
        xb_loaded = [sem(f"xb_loaded{n}") for n in range(2)]
        statsB, rstdB, xnb_ready, xb_biased = sem("statsB"), sem("rstdB"), sem("xnb_ready"), sem("xb_biased")
        xTb_filled, xTb_hi, xTb_read = sem("xTb_filled"), sem("xTb_hi"), sem("xTb_read")
        h_filled, gelu_done, g_hi = sem("h_filled"), sem("gelu_done"), sem("g_hi")
        g_lo = [sem("g_lo_pool"), sem("g_lo_dve")]
        g_used, yb_ready, yb_stored = sem("g_used"), sem("yb_ready"), sem("yb_stored")

        def later(eng, s, value):
            if not isinstance(value, int) or value > 0:
                eng.wait_ge(s, value)

        def g_lo_wait(eng, s, f):
            later(eng, g_lo[f % 2], s * (FC // 2) + f // 2 + 1)

        def steps_b(step_b, eng, chain=None):
            pairs = B // GB // 2
            per = 0
            for slot in range(2):
                n = chain.n if chain else 0
                step_b(slot, slot, 0, True)
                per += chain.n - n if chain else 0
            with eng.Fori(1, pairs - 1) as r:
                if chain:
                    chain.offset = (r - 1) * per
                for slot in range(2):
                    step_b(2 * r + slot, slot, r, True)
            if chain:
                chain.offset = 0
                chain.n += per * (pairs - 3)
            for slot in range(2):
                step_b(2 * (pairs - 1) + slot, slot, pairs - 1, slot == 0)

        def cols(a, s, k):
            return a[:, s, :, k * P:(k + 1) * P]

        def cols4(a, k):
            return a[:, :, k * P:(k + 1) * P]

        def batch_of(i, part):
            return i - {"0": 0, "1f": 1, "1b": 2}[part]

        had_rows = [had[:, 0:P].unsqueeze(1).to_broadcast([P, 4, P]),
                    had[:, 0:2 * P].unsqueeze(1).to_broadcast([P, 2, 2 * P]),
                    had[:, 0:2 * P].rearrange("p (a n) -> p a n", a=2).unsqueeze(2).to_broadcast([P, 2, 2, P]),
                    had]

        def all_read(eng, uses):
            for u in {u.bank: u for u in uses}.values():
                eng.wait_ge(read[u.bank], u.read_at)

        def heads(ap):
            return ap.rearrange("p (h d) -> p h d", h=H)

        block = ctx.enter_context(nc.Block())
        W = [(l, m) for l in range(2) for m in "qkvo"]
        stage_w = [a.rearrange("p (c n) -> p c n", c=DC) for a in (qkT_raw[1][:, 0:DC * D], qkT_raw[1][:, DC * D:2 * DC * D])]
        gt0, tr0 = (a.bitcast(F16).rearrange("p (c n) -> p c n", c=DC)
                    for a in (xn[1].rearrange("p t n -> p (t n)"), xT_raw[1]))
        wb = [qkT_raw[0][:, 0:DC * D], qkT_raw[0][:, DC * D:2 * DC * D]]
        wb_gt = qk_raw[0][:, 0:DC * D // 2].bitcast(F16)
        wb_signs = [qk_raw[0][:, n * DC * D // 2:(n + 1) * DC * D // 2].bitcast(F16) for n in (1, 2)]

        def beside(i, task, *plans):
            return [plan[task] if isinstance(i, int) and i == step and task in plan else None for step, plan in plans]

        split_at = (0, {("stats", 0): 0, ("normalise", 0): 1, ("split_ctx", 0, NT - 1): 2,
                        **{("head", 0, 1 + 2 * n): 3 + n for n in range(len(W) - 3)}})
        tern0_at = (0, {("head", 0, 11): 0})
        turn0_at = (0, {("head", 0, 15): 0})
        mean_at = (B, {("head", 1, 1 + 2 * n): n for n in range(2 * WC)})
        mean_done_at = (B, {("head", 1, 2 * (2 * WC)): 0})
        mean_first_at = (B + 1, {("maxima", 1, EARLY_MAXIMA): 0})
        thresholds_at = (B + 1, {("maxima", 1, H - 1): 0})
        signs_at = (B + 1, {("head", 1, 2 * n): n for n in range(2 * WC)})
        stats_b_at = (B + 1, {("head", 1, 1 + 2 * k): k for k in range(BT)})
        rstd_b_at = (B + 1, {("head", 1, 2 * BT): 0})
        norm_b_at = (B + 1, {("head", 1, 2 * BT + 1 + 2 * k): k for k in range(BT)})
        turn_signs_at = (B + 1, {("head", 1, 2 * n + 4): n for n in range(2 * WC)})

        @block.sync
        def _(sp):
            def load_w(n):
                l, m = W[n]
                if n >= 2:
                    sp.wait_ge(w_split, n - 1)
                w = t[f"L{l}_xattn_W{m}"].rearrange("(c p) n -> p c n", p=P)
                sp.dma_start(stage_w[n % 2][:, 0:w.shape[1], :], w).then_inc(w_loaded[n % 2], 16)

            def load_wb(n):
                if n >= 2:
                    sp.wait_ge(wb_used, n - 1)
                w, c = n % (2 * WC) // WC, n % WC
                src = t["L1_ffn_W1"].rearrange("(a c p) n -> a p c n", a=WC, p=P) if w == 0 else \
                    t["L1_ffn_W2"].rearrange("(a p) n -> a p n", p=P)
                dst = wb[n % 2].rearrange("p (c n) -> p c n", c=FC // WC) if w == 0 else wb[n % 2]
                sp.dma_start(dst, src[c]).then_inc(wb_loaded[n % 2], 16)

            def load(s, slot):
                for g in range(GB):
                    sp.dma_start(Xb[slot][:, g * NT:(g + 1) * NT, :], batch(x2d, s * GB + g)).then_inc(xb_loaded[slot], 16)

            sp.dma_start(X[0], batch(xd, 0)).then_inc(x_loaded[0].sem, 16)
            load_w(0)
            load_w(1)
            sp.dma_start(CT, batch(cd, 0)).then_inc(ctx_loaded.sem, 16)
            for n in row_names:
                sp.dma_start(rows[n], t[n].rearrange("(a n) -> a n", a=1).broadcast_to([P, D])).then_inc(consts_loaded, 16)
            sp.dma_start(had, t["signs"]).then_inc(consts_loaded, 16)
            for n in range(2, len(W)):
                load_w(n)
            sp.wait_ge(w_split, len(W) - 1)
            sp.dma_start(stage_w[0], t["L0_ffn_weight"].rearrange("(c p) n -> p c n", p=P)).then_inc(w_loaded[0], 16)

            def step(active, i, use):
                if "0" in active and not (isinstance(i, int) and i == 0):
                    sp.wait_ge(xp_ready.sem, xp_ready.at(i - 1))
                    sp.dma_start(X[0], batch(xd, i)).then_inc(x_loaded[0].sem, 16)
                    sp.dma_start(CT, batch(cd, i)).then_inc(ctx_loaded.sem, 16)
                if isinstance(i, int) and i == B:
                    sp.wait_ge(x1_stored.sem, x1_stored.at(B - 1))
                    sp.dma_start(b2_row, t["L1_ffn_b2"].rearrange("(a n) -> a n", a=1).broadcast_to([P, D])).then_inc(biasb_loaded, 16)
                    sp.dma_start(b1c, t["L1_ffn_b1"].rearrange("(c p) -> p c", p=P),
                                 allow_slow_non_contiguous=True).then_inc(biasb_loaded, 16)
                if isinstance(i, int) and i >= B:
                    for n in range(2 * WC):
                        load_wb((i - B) * 2 * WC + n)
                if "1b" in active:
                    for k in range(NT):
                        sp.wait_ge(read[use["y", 1, k].bank], use["y", 1, k].read_at)
                    sp.dma_start(batch(x2d, i - 2), X[1]).then_inc(x2_stored.sem, 16)
                if "1f" in active:
                    if not (isinstance(i, int) and i == 1):
                        sp.wait_ge(x2_stored.sem, x2_stored.at(i - 2))
                    sp.wait_ge(x1_stored.sem, x1_stored.at(i - 1))
                    sp.dma_start(X[1], batch(x1d, i - 1)).then_inc(x_loaded[1].sem, 16)
                    if isinstance(i, int) and i == B:
                        u = use["qkv", 1, NT - 1, 0]
                        sp.wait_ge(filled[u.bank], u.filled_at)
                        load(0, 0)
                if "0" in active:
                    for k in range(NT):
                        sp.wait_ge(read[use["c", 0, k].bank], use["c", 0, k].read_at)
                    if "1f" in active:
                        u = use["qkv", 1, NT - 1, 2]
                        sp.wait_ge(filled[u.bank], u.filled_at)
                    sp.dma_start(cT_raw[1], cT_raw[0]).then_inc(ctxT_copied.sem, 16)

            steps(sp, step)

            def store(s, slot):
                sp.wait_ge(yb_ready, s * BT + BT)
                for g in range(GB):
                    sp.dma_start(batch(od, s * GB + g), Xb[slot][:, g * NT:(g + 1) * NT, :]).then_inc(yb_stored, 16)

            sp.wait_ge(x2_stored.sem, x2_stored.at(B - 1))
            load(1, 1)
            with sp.Fori(0, B // GB // 2 - 1) as r:
                for slot in range(2):
                    s = 2 * r + slot
                    store(s, slot)
                    sp.wait_ge(yb_stored, s * (16 * GB) + 16 * GB)
                    load(s + 2, slot)
            for slot in range(2):
                store(B // GB - 2 + slot, slot)
            sp.wait_ge(yb_stored, 16 * B)

        @block.gpsimd
        def _(pool):
            chain = Chain(pool, pool_step)
            gp = nc.gpsimd
            gp.memset(ident, 0.0).then_inc(const_ready, 1)
            gp.memset(identh, 0.0).then_inc(const_ready, 1)
            pool.wait_ge(const_ready, 2)
            for m in (ident, identh):
                gp.affine_select(out=m, in_=m, compare_op=ALU.not_equal, fill=1.0, base=0,
                                 pattern=[[-1, P]], channel_multiplier=1).then_inc(const_ready, 1)
            for ap, value in ((half4, -0.5), (eps4, EPS), (qs4, QS), (had4, HAD)):
                gp.memset(ap, value).then_inc(const_ready, 1)
            gp.memset(one4, -1.0).then_inc(const_ready, 1)
            gp.memset(magic, MAGIC).then_inc(const_ready, 1)
            gp.memset(one_col, 1.0).then_inc(const_ready, 1)
            for l in range(2):
                gp.memset(vs[l][:, :, :, HD:HD + 2], 1.0).then_inc(const_ready, 1)
            pool.wait_ge(const_ready, CONSTS)
            pool.wait_ge(consts_loaded, 16 * (len(row_names) + 1))

            def rstd(name, ts):
                at = slice(ts[0], ts[0] + len(ts))
                chain(gp.tensor_tensor(tmp[name][:, at], mv[name][:, at, 1], eps4[:, at], ALU.add))
                return gp.tensor_tensor(rs[name][:, at], tmp[name][:, at], half4[:, at], ALU.pow)

            def prep_b(s):
                pool.wait_ge(statsB, s * BT + BT)
                chain(gp.tensor_tensor(tmp["B"], mv["B"][:, :, 1], eps4, ALU.add))
                gp.tensor_tensor(rs["B"], tmp["B"], half4, ALU.pow).then_inc(rstdB, 1)

            def step(active, i, use):
                for part, (kind, l, *at) in task_order(active):
                    b = batch_of(i, part)
                    if kind == "stats":
                        pool.wait_ge(stats_A[l].sem, stats_A[l].at(b))
                        rstd(f"A{l}", [0, 1]).then_inc(rstd_A[l].sem, 1)
                    elif kind == "normalise":
                        pool.wait_ge(xn_ready[l].sem, xn_ready[l].at(b))
                        bias = rows["L0_xattn_ln_beta" if l == 0 else "L1_xattn_bo"]
                        gp.tensor_tensor(X[l], X[l], bias.unsqueeze(1).to_broadcast([P, NT, D]), ALU.add).then_inc(xbias[l].sem, 1)
                    elif kind == "bias" and at[1] == 2:
                        k = at[0]
                        vf = vf0[k] if l == 0 else kv1[:, 2 * D:3 * D]
                        pool.wait_ge(v_hi[l].sem, v_hi[l].at(b, k + 1))
                        gp.tensor_tensor(vs[l][:, k, :, HD + 2:VP], heads(vf), vs[l][:, k, :, 0:HD],
                                         ALU.subtract).then_inc(v_lo[l].sem, 1)
                    elif kind == "norm" and l == 0:
                        c = slice(2 * at[0], 2 * at[0] + 2)
                        pool.wait_ge(guarded.sem, guarded.at(b, at[0] + 1))
                        chain(gp.tensor_tensor(tmp["N"][:, c], ssq[:, c], half4[:, c], ALU.pow))
                        gp.tensor_tensor(rn[:, c], tmp["N"][:, c], qs4[:, c], ALU.mult).then_inc(norms.sem, 1)
                    elif kind == "lower_qk" and l == 0 and at[0] == NT - 1:
                        pool.wait_ge(qk_hi[0].sem, qk_hi[0].at(b))
                        pool.wait_ge(qk_lo[0].sem, qk_lo[0].at(b))
                        gp.tensor_tensor(qf0, qf0, rows["L0_xattn_bo"].unsqueeze(1).to_broadcast([P, NT, D]),
                                         ALU.add).then_inc(qf_biased.sem, 1)
                    elif kind == "head":
                        h = at[0] - 1 - l
                        if 0 <= h < H:
                            u = use["s", l, h]
                            pool.wait_ge(read[u.bank], u.read_at)
                            pool.wait_ge(p_hi[l].sem, p_hi[l].at(b, h + 1))
                            gp.tensor_tensor(pl[l][:, h % NP, :], pf[l][h % 2], ph[l][:, h % NP, :],
                                             ALU.subtract).then_inc(p_lo[l].sem, 1)
                    elif kind == "out" and l == 0:
                        pool.wait_ge(stats_E.sem, stats_E.at(b, at[0] + 1))
                        rstd("E", at).then_inc(rstd_E.sem, 1)
                    elif kind == "post_norm":
                        pool.wait_ge(stats_F.sem, stats_F.at(b, at[0] + 1))
                        rstd("F", at).then_inc(rstd_F.sem, 1)
                    elif kind == "absmax":
                        k = at[0]
                        pool.wait_ge(absmax.sem, absmax.at(b, k + 1))
                        chain(gp.tensor_tensor(tmp["Q"][:, k:k + 1], qsc[:, k:k + 1], one4[:, 0:1], ALU.pow))
                        gp.tensor_tensor(qrs[:, k:k + 1], tmp["Q"][:, k:k + 1], had4[:, 0:1], ALU.mult).then_inc(qscale.sem, 1)
                    elif kind == "ffn0_out":
                        k = at[0]
                        u = use["f0", 0, k]
                        pool.wait_ge(read[u.bank], u.read_at)
                        gp.tensor_tensor(tq[k], tq[k], xp[:, k, :], ALU.add).then_inc(x1_ready.sem, 1)
                    elif kind == "store_x1":
                        pool.wait_ge(x1_ready.sem, x1_ready.at(b))
                        pool.dma_start(batch(x1d, b), kv0[:, 0:2 * D].rearrange("p (t n) -> p t n", t=NT)).then_inc(x1_stored.sem, 16)
                    if beside(i, (kind, l, *at), rstd_b_at)[0] is not None:
                        prep_b(0)

            steps(pool, step, chain)

            def bias_b(s, slot):
                pool.wait_ge(xnb_ready, s * BT + BT)
                gp.tensor_tensor(Xb[slot], Xb[slot], b2_row.unsqueeze(1).to_broadcast([P, BT, D]), ALU.add).then_inc(xb_biased, 1)

            def step_b(s, slot, r, has_next):
                for f in range(FC):
                    if f % 2 == 0:
                        pool.wait_ge(g_hi, s * FC + f + 1)
                        gp.tensor_tensor(gl[:, f % NG, :], gf[f % 2], gh[:, f % NG, :], ALU.subtract).then_inc(g_lo[0], 1)
                    if f == NORM_AT - 1 and has_next:
                        prep_b(s + 1)
                    if f == FC - 2 and has_next:
                        bias_b(s + 1, 1 - slot)

            bias_b(0, 0)
            steps_b(step_b, pool, chain)

        @block.scalar
        def _(act):
            sc = nc.scalar
            act.wait_ge(const_ready, CONSTS)

            def split_weight(n):
                c = wsplit[W[n]].shape[2]
                act.wait_ge(w_loaded[n % 2], 16 * (n // 2 + 1))
                sc.activation(wsplit[W[n]][:, 0], stage_w[n % 2][:, 0:c, :], ACT.Copy, scale=WS).then_inc(w_hi, 1)

            def copy_tern0():
                act.wait_ge(setup_pe, 1)
                sc.activation(wsc_row, bank(0), ACT.Copy).then_inc(setup_act, 1)
                for c in range(DC):
                    act.wait_ge(setup_pe, c + 2)
                    sc.activation(tern0[:, c, :], bank((c + 1) % 4).bitcast(F16)[:, 0:D], ACT.Copy).then_inc(setup_act, 1)

            def copy_signs(n):
                w, c = n // WC, n % WC
                for g in range(2):
                    act.wait_ge(wtr_filled, 2 * n + g + 1)
                    src = bank(g).bitcast(F16)
                    if w == 0:
                        sc.activation(w1T[:, 2 * g:2 * g + 2, c * (FF // WC):(c + 1) * (FF // WC)],
                                      src.rearrange("p (d n) -> p d n", d=2), ACT.Copy).then_inc(wtr_read, 1)
                    else:
                        sc.activation(w2T[:, g * 8:(g + 1) * 8, c * P:(c + 1) * P], src.rearrange("p (f n) -> p f n", f=8),
                                      ACT.Copy).then_inc(wtr_read, 1)

            def twice(ap):
                return heads(ap).unsqueeze(2).to_broadcast([P, H, 2, HD])

            def hi(src_use, dst, sig):
                act.wait_ge(filled[src_use.bank], src_use.filled_at)
                n = dst.shape[1]
                sc.activation(dst, bank(src_use.bank)[:, 0:n * P].rearrange("p (c n) -> p c n", c=n), ACT.Copy).then_inc(sig, 1)

            def step(active, i, use):
                for part, (kind, l, *at) in task_order(active):
                    b = batch_of(i, part)
                    if kind == "turn_x":
                        hi(use["x", l, at[0]], cols(xT[l], 0, at[0]), xT_hi[l].sem)
                    elif kind == "turn_ctx":
                        if at[0] == 0 and not (isinstance(i, int) and i == 0):
                            act.wait_ge(ctxT_copied.sem, ctxT_copied.at(i - 1))
                        hi(use["c", 0, at[0]], cols(cT[0], 0, at[0]), ctxT_hi.sem)
                    elif kind == "bias" and l == 0 and at[1] < 2:
                        k, j = at
                        u = use["qkv", 0, k, j]
                        act.wait_ge(read[u.bank], u.read_at)
                        if j + 2 * k:
                            act.wait_ge(squares.sem, squares.at(b, 2 * k + j))
                        sc.activation(xn[0][:, 0, :], (qf0[:, k, :], kf0[k])[j], ACT.Square,
                                      accum_out=ssq[:, 2 * k + j:2 * k + j + 1]).then_inc(squares.sem, 1)
                    elif kind == "upper_qk":
                        k = at[0]
                        if l == 0:
                            act.wait_ge(norms.sem, norms.at(b, k + 1))
                        for j in range(2):
                            if l == 0:
                                sc.activation(qk_hi_of(0, j, k), twice((qf0[:, k, :], kf0[k])[j]), ACT.Copy,
                                              scale=rn[:, 2 * k + j:2 * k + j + 1]).then_inc(qk_hi[0].sem, 1)
                            else:
                                u = use["qkv", 1, k, j]
                                act.wait_ge(read[u.bank], u.read_at)
                                sc.activation(qk_hi_of(1, j, k), twice(kv1[:, j * D:(j + 1) * D]), ACT.Copy).then_inc(qk_hi[1].sem, 1)
                    elif kind == "stack":
                        k, j, g = at
                        if l == 1 and k + j + g == 0:
                            act.wait_ge(qk_lo[1].sem, qk_lo[1].at(b))
                            act.wait_ge(v_lo[1].sem, v_lo[1].at(b))
                        u = use["st", l, k, j, g]
                        act.wait_ge(filled[u.bank], u.filled_at)
                        sc.activation(qkT[l][0:QW, j, g * 8:(g + 1) * 8, k * P:(k + 1) * P],
                                      bank(u.bank).bitcast(F16)[0:QW].rearrange("p (h n) -> p h n", h=8),
                                      ACT.Copy).then_inc(read[u.bank], 1)
                    elif kind == "head" and 0 <= at[0] - l < H:
                        h = at[0] - l
                        u = use["s", l, h]
                        if l == 0:
                            act.wait_ge(filled[u.bank], u.filled_at)
                            if h == 0:
                                act.wait_ge(v_lo[0].sem, v_lo[0].at(b))
                        else:
                            act.wait_ge(shifted.sem, shifted.at(b, h + 1))
                        if h >= 2:
                            act.wait_ge(p_lo[l].sem, p_lo[l].at(b, h - 1))
                        sc.activation(pf[l][h % 2], bank(u.bank), ACT.Exp,
                                      scale=SCALE / (QS * QS) if l == 0 else SCALE).then_inc(read[u.bank], 1)
                    elif kind == "turn_out":
                        hi(use["ot", l, at[0]], cols(xT[l], 0, at[0]), oT_hi[l].sem)
                    elif kind == "turn_ffn":
                        hi(use["xf", 0, at[0]], cols(xT[0], 0, at[0]), xF_hi.sem)
                    elif kind == "round":
                        k = at[0]
                        act.wait_ge(qscale.sem, qscale.at(b, k + 1))
                        u = use["had", 0, k]
                        sc.activation(tq[k], bank(u.bank), ACT.Identity, bias=magic, scale=qrs[:, k:k + 1]).then_inc(read[u.bank], 1)
                    elif kind == "turn_levels":
                        k = at[0]
                        u = use["nt", 0, k]
                        act.wait_ge(filled[u.bank], u.filled_at)
                        sc.activation(cols4(nT, k), bank(u.bank).bitcast(F16)[:, 0:D].rearrange("p (c n) -> p c n", c=DC),
                                      ACT.Copy).then_inc(read[u.bank], 1)
                    weight, tern, signs = beside(i, (kind, l, *at), split_at, turn0_at, turn_signs_at)
                    if weight is not None:
                        split_weight(weight)
                    if tern is not None:
                        copy_tern0()
                    if signs is not None:
                        copy_signs(signs)

            steps(act, step)

            act.wait_ge(biasb_loaded, 32)

            def upper_b(s, slot, k):
                act.wait_ge(xTb_filled, s * BT + k + 1)
                sc.activation(xTb[slot][:, 0, :, k * P:(k + 1) * P], bank(6 + k % 2).rearrange("p (c n) -> p c n", c=DC),
                              ACT.Copy).then_inc(xTb_hi, 1)

            def step_b(s, slot, r, has_next):
                for f in range(FC):
                    act.wait_ge(h_filled, s * FC + f + 1)
                    g_lo_wait(act, s, f - 2)
                    sc.activation(gf[f % 2], bank(4 + f % 2), ACT.Gelu, bias=b1c[:, f:f + 1]).then_inc(gelu_done, 1)
                    k = f - TURN_AT - 1
                    if has_next and 0 <= k < BT:
                        upper_b(s + 1, 1 - slot, k)

            for k in range(BT):
                upper_b(0, 0, k)
            steps_b(step_b, act)

        @block.vector
        def _(dve):
            chain = Chain(dve, dve_step)
            v = nc.vector
            dve.wait_ge(const_ready, CONSTS)

            def split_weight(n):
                c = wsplit[W[n]].shape[2]
                dve.wait_ge(w_hi, n + 1)
                v.scalar_tensor_tensor(out=wsplit[W[n]][:, 1], in0=stage_w[n % 2][:, 0:c, :], scalar=WS,
                                       in1=wsplit[W[n]][:, 0], op0=ALU.mult, op1=ALU.subtract).then_inc(w_split, 1)

            def tern0_signs():
                dve.wait_ge(w_loaded[0], 16 * (len(W) // 2 + 1))
                chain(v.tensor_reduce(wthr[:, 0:DC], stage_w[0], AX_X, ALU.add, apply_absolute_value=True))
                chain(v.tensor_scalar(wsum_rows, wthr[:, 0:DC], 1.0 / D, 1e-5, ALU.mult, ALU.max))
                v.tensor_scalar(wthr[:, 0:DC], wsum_rows, 0.5, None, ALU.mult).then_inc(setup_dve, 1)
                v.tensor_scalar(wthr[:, DC:2 * DC], wsum_rows, -0.5, None, ALU.mult).then_inc(setup_dve, 1)
                dve.wait_ge(setup_dve, 2)
                for c in range(DC):
                    v.tensor_scalar(gt0[:, c, :], stage_w[0][:, c, :], wthr[:, DC + c:DC + c + 1], None, ALU.is_lt).then_inc(dve_step, 1)
                    chain.n += 1
                dve.wait_ge(dve_step, chain.n)
                for c in range(DC):
                    v.scalar_tensor_tensor(out=tr0[:, c, :], in0=stage_w[0][:, c, :], scalar=wthr[:, c:c + 1],
                                           in1=gt0[:, c, :], op0=ALU.is_gt, op1=ALU.subtract).then_inc(setup_dve, 1)

            def mean_part(n):
                dve.wait_ge(wb_loaded[n % 2], 16 * (n // 2 + 1))
                v.tensor_reduce(wab[:, n:n + 1], wb[n % 2], AX_X, ALU.add, apply_absolute_value=True).then_inc(wb_used, 1)

            def thresholds():
                dve.wait_ge(wb_sum, 1)
                chain(v.tensor_scalar(wthr[:, 0:2], bank(0)[:, 0:2], 1.0 / (D * FF), 1e-8, ALU.mult, ALU.max))
                chain(v.tensor_scalar(wthr[:, 2:4], wthr[:, 0:2], 0.5, None, ALU.mult))
                chain(v.tensor_scalar(wthr[:, 4:6], wthr[:, 0:2], -0.5, None, ALU.mult))

            def signs_of(n):
                w, m = n // WC, 2 * WC + n
                dve.wait_ge(wb_loaded[m % 2], 16 * (m // 2 + 1))
                chain(v.tensor_scalar(wb_gt, wb[m % 2], wthr[:, 4 + w:5 + w], None, ALU.is_lt))
                if n >= 2:
                    dve.wait_ge(wtr_filled, 2 * n - 2)
                v.scalar_tensor_tensor(out=wb_signs[n % 2], in0=wb[m % 2], scalar=wthr[:, 2 + w:3 + w], in1=wb_gt,
                                       op0=ALU.is_gt, op1=ALU.subtract).then_inc(wb_used, 1)
                dve.wait_ge(wb_used, m + 1)

            def ln_stats(name, src, k, sig):
                v.bn_stats(st[:, 6 * k:6 * k + 6], src)
                dve.drain()
                v.bn_aggr(mv[name][:, k, :], st[:, 6 * k:6 * k + 6]).then_inc(sig, 1)

            def normalise(name, dst, src, k, sig):
                v.tensor_scalar(dst, src, mv[name][:, k, 0:1], rs[name][:, k:k + 1], ALU.subtract, ALU.mult).then_inc(sig, 1)

            def lo(u, dst, upper, hi_sig, value):
                dve.wait_ge(hi_sig, value)
                n = dst.shape[1]
                v.tensor_tensor(dst, bank(u.bank)[:, 0:n * P].rearrange("p (c n) -> p c n", c=n), upper,
                                ALU.subtract).then_inc(read[u.bank], 1)

            def stats_b(s, slot, r, k):
                if k == 0:
                    dve.wait_ge(xb_loaded[slot], r * (16 * GB) + 16 * GB)
                ln_stats("B", Xb[slot][:, k, :], k, statsB)

            def norm_b(s, slot, k):
                if k == 0:
                    dve.wait_ge(rstdB, s + 1)
                    dve.wait_ge(statsB, s * BT + BT)
                normalise("B", xnb[:, k, :], Xb[slot][:, k, :], k, xnb_ready)

            def step(active, i, use):
                first = isinstance(i, int) and i == 0
                for part, (kind, l, *at) in task_order(active):
                    b = batch_of(i, part)
                    k = at[0] if at else None
                    if kind == "stats":
                        dve.wait_ge(x_loaded[l].sem, x_loaded[l].at(b))
                        for k in range(NT):
                            ln_stats(f"A{l}", X[l][:, k, :], k, stats_A[l].sem)
                    elif kind == "normalise":
                        dve.wait_ge(rstd_A[l].sem, rstd_A[l].at(b))
                        dve.wait_ge(stats_A[l].sem, stats_A[l].at(b))
                        for k in range(NT):
                            normalise(f"A{l}", xn[l][:, k, :], X[l][:, k, :], k, xn_ready[l].sem)
                    elif kind == "split_x":
                        lo(use["x", l, k], cols(xT[l], 1, k), cols(xT[l], 0, k), xT_hi[l].sem, xT_hi[l].at(b, k + 1))
                    elif kind == "split_ctx":
                        if k == 0 and not first:
                            dve.wait_ge(ctxT_copied.sem, ctxT_copied.at(i - 1))
                        lo(use["c", 0, k], cols(cT[0], 1, k), cols(cT[0], 0, k), ctxT_hi.sem, ctxT_hi.at(b, k + 1))
                    elif kind == "bias":
                        j = at[1]
                        if l == 0 and first and k + j == 0:
                            dve.wait_ge(consts_loaded, 16 * (len(row_names) + 1))
                        if l == 0 and not first and k + j == 0:
                            dve.wait_ge(x1_stored.sem, x1_stored.at(i - 1))
                        u = use["qkv", l, k, j]
                        if l == 0:
                            dst = (qf0[:, k, :], kf0[k], vf0[k])[j]
                        else:
                            dst = kv1[:, j * D:(j + 1) * D]
                            if k and j < 2:
                                dve.wait_ge(qk_lo[1].sem, qk_lo[1].at(b, 2 * (k - 1) + j + 1))
                            elif k:
                                dve.wait_ge(v_lo[1].sem, v_lo[1].at(b, k))
                        dve.wait_ge(filled[u.bank], u.filled_at)
                        v.scalar_tensor_tensor(out=dst, in0=bank(u.bank), scalar=1.0 / WS, in1=rows[f"L{l}_xattn_b{'qkv'[j]}"],
                                               op0=ALU.mult, op1=ALU.add).then_inc(read[u.bank], 1)
                        if j == 2:
                            dve.wait_ge(read[u.bank], u.read_at)
                            v.tensor_copy(vs[l][:, k, :, 0:HD], heads(dst)).then_inc(v_hi[l].sem, 1)
                    elif kind == "norm" and l == 0:
                        c = slice(2 * k, 2 * k + 2)
                        dve.wait_ge(squares.sem, squares.at(b, 2 * k + 2))
                        v.tensor_scalar(ssq[:, c], ssq[:, c], 1e-24, None, ALU.max).then_inc(guarded.sem, 1)
                    elif kind == "lower_qk":
                        for j in range(2):
                            dve.wait_ge(qk_hi[l].sem, qk_hi[l].at(b, 2 * k + j + 1))
                            if l == 0:
                                v.scalar_tensor_tensor(out=qk_lo_of(0, j, k), in0=heads((qf0[:, k, :], kf0[k])[j]),
                                                       scalar=rn[:, 2 * k + j:2 * k + j + 1], in1=qk_one_hi_of(0, j, k),
                                                       op0=ALU.mult, op1=ALU.subtract).then_inc(qk_lo[0].sem, 1)
                            else:
                                v.tensor_tensor(qk_lo_of(1, j, k), heads(kv1[:, j * D:(j + 1) * D]),
                                                qk_one_hi_of(1, j, k), ALU.subtract).then_inc(qk_lo[1].sem, 1)
                    elif kind == "maxima":
                        u = use["mx", 1, k]
                        dve.wait_ge(filled[u.bank], u.filled_at)
                        v.tensor_reduce(mx[:, :, k], bank(u.bank).rearrange("p (t n) -> p t n", t=NT), AX_X,
                                        ALU.max).then_inc(read[u.bank], 1)
                    elif kind == "shifts":
                        all_read(dve, [use["mx", 1, h] for h in range(EARLY_MAXIMA, H)])
                        chain(v.tensor_scalar(mx, mx, CLAMP / SCALE, -CLAMP / SCALE, ALU.min, ALU.max))
                        v.tensor_scalar(mneg, mx, -1.0, None, ALU.mult).then_inc(shift_ready.sem, 1)
                    elif kind == "head":
                        n = k
                        h = n - 1 - l
                        if 0 <= h < H and not UPPER_ON_ACT[l]:
                            u = use["s", l, h]
                            dve.wait_ge(read[u.bank], u.read_at)
                            if h >= NP:
                                dve.wait_ge(av_done[l].sem, av_done[l].at(b, h + 1 - NP))
                            v.tensor_copy(ph[l][:, h % NP, :], pf[l][h % 2]).then_inc(p_hi[l].sem, 1)
                        if l == 1 and n < H:
                            u = use["s", 1, n]
                            dve.wait_ge(filled[u.bank], u.filled_at)
                            v.tensor_scalar(bank(u.bank), bank(u.bank), CLAMP / SCALE, -CLAMP / SCALE, ALU.min,
                                            ALU.max).then_inc(clipped.sem, 1)
                        h = n - AV_LAG[l] - 1
                        if 0 <= h < H and h % HG == HG - 1:
                            attn_out(l, b, h // HG, use)
                    elif kind == "split_out":
                        lo(use["ot", l, k], cols(xT[l], 1, k), cols(xT[l], 0, k), oT_hi[l].sem, oT_hi[l].at(b, k + 1))
                    elif kind == "out":
                        u = use["y", l, k]
                        if k == 0:
                            dve.wait_ge(xbias[l].sem, xbias[l].at(b))
                            if l == 0:
                                dve.wait_ge(qf_biased.sem, qf_biased.at(b))
                        dve.wait_ge(filled[u.bank], u.filled_at)
                        if l == 1:
                            v.scalar_tensor_tensor(out=X[1][:, k, :], in0=bank(u.bank), scalar=1.0 / WS, in1=X[1][:, k, :],
                                                   op0=ALU.mult, op1=ALU.add).then_inc(read[u.bank], 1)
                        else:
                            v.scalar_tensor_tensor(out=yf[k], in0=bank(u.bank), scalar=1.0 / WS, in1=qf0[:, k, :],
                                                   op0=ALU.mult, op1=ALU.add).then_inc(read[u.bank], 1)
                            dve.wait_ge(read[u.bank], u.read_at)
                            ln_stats("E", yf[k], k, stats_E.sem)
                    elif kind == "post_norm":
                        dve.wait_ge(rstd_E.sem, rstd_E.at(b, k + 1))
                        chain(v.scalar_tensor_tensor(out=yf[k], in0=yf[k], scalar=mv["E"][:, k, 0:1],
                                                     in1=rows["L0_xattn_ln_gamma"], op0=ALU.subtract, op1=ALU.mult))
                        v.scalar_tensor_tensor(out=xp[:, k, :], in0=yf[k], scalar=rs["E"][:, k:k + 1], in1=X[0][:, k, :],
                                               op0=ALU.mult, op1=ALU.add).then_inc(xp_ready.sem, 1)
                        dve.wait_ge(xp_ready.sem, xp_ready.at(b, k + 1))
                        ln_stats("F", xp[:, k, :], k, stats_F.sem)
                    elif kind == "normalise_ffn":
                        dve.wait_ge(rstd_F.sem, rstd_F.at(b, k + 1))
                        normalise("F", xn[0][:, k, :], xp[:, k, :], k, xnF_ready.sem)
                    elif kind == "split_ffn":
                        lo(use["xf", 0, k], cols(xT[0], 1, k), cols(xT[0], 0, k), xF_hi.sem, xF_hi.at(b, k + 1))
                    elif kind == "absmax":
                        u = use["had", 0, k]
                        dve.wait_ge(filled[u.bank], u.filled_at)
                        chain(v.tensor_reduce(am[:, k:k + 1], bank(u.bank), AX_X, ALU.max, apply_absolute_value=True))
                        chain(v.tensor_scalar(am[:, k:k + 1], am[:, k:k + 1], HAD, 1e-5, ALU.mult, ALU.max))
                        v.tensor_scalar(qsc[:, k:k + 1], am[:, k:k + 1], 1.0 / 7.0, None, ALU.mult).then_inc(absmax.sem, 1)
                    elif kind == "levels":
                        u = use["had", 0, k]
                        dve.wait_ge(read[u.bank], u.read_at)
                        v.tensor_scalar(nq[:, k, :], tq[k], MAGIC, 7.0, ALU.subtract, ALU.min).then_inc(nq_ready.sem, 1)
                    elif kind == "ffn0_out":
                        u = use["f0", 0, k]
                        dve.wait_ge(filled[u.bank], u.filled_at)
                        v.scalar_tensor_tensor(out=tq[k], in0=bank(u.bank), scalar=qsc[:, k:k + 1], in1=wsc_row,
                                               op0=ALU.mult, op1=ALU.mult).then_inc(read[u.bank], 1)
                    weight, tern, mean, mean_done, thr, signs, stats, norm = beside(
                        i, (kind, l, *at), split_at, tern0_at, mean_at, mean_done_at, thresholds_at, signs_at,
                        stats_b_at, norm_b_at)
                    if weight is not None:
                        split_weight(weight)
                    if tern is not None:
                        tern0_signs()
                    if mean is not None:
                        mean_part(mean)
                    if mean_done is not None:
                        dve.wait_ge(wb_used, 2 * WC)
                        v.tensor_reduce(wsum, wab.rearrange("p (w c) -> p w c", w=2), AX_X, ALU.add).then_inc(wb_part, 1)
                    if thr is not None:
                        thresholds()
                    if signs is not None:
                        signs_of(signs)
                    if stats is not None:
                        stats_b(0, 0, 0, stats)
                    if norm is not None:
                        norm_b(0, 0, norm)

            def attn_out(l, b, g, use):
                u = use["o", l, g]
                if g:
                    dve.wait_ge(read[use["o", l, g - 1].bank], use["o", l, g - 1].read_at)
                dve.wait_ge(av_done[l].sem, av_done[l].at(b, (g + 1) * HG))
                o = bank(u.bank)[:, 0:NT * HG * OW].rearrange("p (t h d) -> p t h d", t=NT, h=HG)
                chain(v.reciprocal(rden[l], o[:, :, :, HD]))
                dst = xn[l].rearrange("p t (h d) -> p t h d", h=H)[:, :, g * HG:(g + 1) * HG, :]
                for k in range(NT):
                    ins = v.tensor_tensor(dst[:, k], o[:, k, :, 0:HD], rden[l][:, k, :].unsqueeze(2).to_broadcast([P, HG, HD]), ALU.mult)
                    if k == NT - 1:
                        ins.then_inc(read[u.bank], 1)

            steps(dve, step, chain)

            def add_b(s, slot):
                dve.wait_ge(xb_biased, s + 1)
                dve.wait_ge(g_used, s * FC + FC)
                for k in range(BT):
                    v.tensor_tensor(Xb[slot][:, k, :], bank(k), Xb[slot][:, k, :], ALU.add).then_inc(yb_ready, 1)

            def split_b(s, slot, k):
                dve.wait_ge(xTb_hi, s * BT + k + 1)
                v.tensor_tensor(xTb[slot][:, 1, :, k * P:(k + 1) * P], bank(6 + k % 2).rearrange("p (c n) -> p c n", c=DC),
                                xTb[slot][:, 0, :, k * P:(k + 1) * P], ALU.subtract).then_inc(xTb_read, 1)

            def step_b(s, slot, r, has_next):
                for f in range(FC):
                    dve.wait_ge(gelu_done, s * FC + f + 1)
                    later(dve, g_used, s * FC + f + 1 - NG)
                    v.tensor_copy(gh[:, f % NG, :], gf[f % 2]).then_inc(g_hi, 1)
                    if f == 0 and not (isinstance(s, int) and s == 0):
                        add_b(s - 1, 1 - slot)
                    if f % 2:
                        dve.wait_ge(g_hi, s * FC + f + 1)
                        v.tensor_tensor(gl[:, f % NG, :], gf[f % 2], gh[:, f % NG, :], ALU.subtract).then_inc(g_lo[1], 1)
                    if has_next:
                        if 0 <= f - STATS_AT < BT:
                            stats_b(s + 1, 1 - slot, r + slot, f - STATS_AT)
                        if 0 <= f - NORM_AT < BT:
                            norm_b(s + 1, 1 - slot, f - NORM_AT)
                        if 0 <= f - TURN_AT - 2 < BT:
                            split_b(s + 1, 1 - slot, f - TURN_AT - 2)
            for k in range(BT):
                split_b(0, 0, k)
            steps_b(step_b, dve, chain)
            add_b(B // GB - 1, (B // GB - 1) % 2)

        @block.tensor
        def _(pe):
            te = nc.tensor
            pe.wait_ge(const_ready, CONSTS)

            def turn_tern0():
                pe.wait_ge(setup_dve, DC + 2)
                for c in range(DC):
                    mm = te.matmul(bank(0)[:, c * P:(c + 1) * P], wsum_rows[:, c:c + 1].to_broadcast([P, P]), ident,
                                   start=True, stop=True)
                mm.then_inc(setup_pe, 1)
                for c in range(DC):
                    if c == DC - 1:
                        pe.wait_ge(setup_act, 1)
                    for o in range(DC):
                        mm = te.transpose(bank((c + 1) % 4).bitcast(F16)[:, o * P:(o + 1) * P], tr0[:, o, c * P:(c + 1) * P], identh)
                    mm.then_inc(setup_pe, 1)

            def mean_all():
                pe.wait_ge(wb_part, 1)
                te.matmul(bank(0)[:, 0:2], one_col.to_broadcast([P, P]), wsum, start=True, stop=True).then_inc(wb_sum, 1)

            def turn_signs(n):
                w = n // WC
                pe.wait_ge(wb_used, 2 * WC + n + 1)
                for g in range(2):
                    later(pe, wtr_read, 2 * n + g - 1)
                    for x in range(8):
                        col = ((x % 4) * DC + 2 * g + x // 4) * P if w == 0 else (g * 8 + x) * P
                        mm = te.transpose(bank(g).bitcast(F16)[:, x * P:(x + 1) * P], wb_signs[n % 2][:, col:col + P], identh)
                    mm.then_inc(wtr_filled, 1)

            def open_bank(u):
                if not (isinstance(u.free_at, int) and u.free_at == 0):
                    pe.wait_ge(read[u.bank], u.free_at)

            def product(out, lhs, w, k, chunks, first=0, last=None):
                for c in range(first, chunks if last is None else last):
                    x_hi, x_lo = (lhs[:, s, c, k * P:(k + 1) * P] for s in range(2))
                    te.matmul(out, x_hi, w[:, 0, c, :], start=(c == 0), stop=False)
                    te.matmul(out, x_hi, w[:, 1, c, :], start=False, stop=False)
                    mm = te.matmul(out, x_lo, w[:, 0, c, :], start=False, stop=(c == chunks - 1))
                return mm

            def turn(u, src, chunks):
                open_bank(u)
                for c in range(chunks):
                    mm = te.transpose(bank(u.bank)[:, c * P:(c + 1) * P], src[:, c * P:(c + 1) * P], ident)
                mm.then_inc(filled[u.bank], 1)

            def step(active, i, use):
                for part, (kind, l, *at) in task_order(active):
                    b = batch_of(i, part)
                    k = at[0] if at else None
                    if kind == "turn_x":
                        pe.wait_ge(xn_ready[l].sem, xn_ready[l].at(b, k + 1))
                        turn(use["x", l, k], xn[l][:, k, :], DC)
                    elif kind == "turn_ctx":
                        if k == 0:
                            pe.wait_ge(ctx_loaded.sem, ctx_loaded.at(b))
                        turn(use["c", 0, k], CT[:, k, :], CC)
                    elif kind == "project":
                        j, late = at[1:]
                        u = use["qkv", l, k, j]
                        if isinstance(i, int) and i == l and k + late == 0:
                            pe.wait_ge(w_split, j + 1 if l == 0 else len(W))
                        if late == 0:
                            if j == 0:
                                all_read(pe, [use["x", l, k]] + ([use["c", 0, k]] if l == 0 else []))
                                if l == 1 and k == 0:
                                    pe.wait_ge(ctxT_copied.sem, ctxT_copied.at(b))
                            open_bank(u)
                        src, n = (xT[l], DC) if j == 0 else (cT[l], CC)
                        mm = product(bank(u.bank), src, wsplit[l, "qkv"[j]], k, n, 2 * late, n if late else 2)
                        if late:
                            mm.then_inc(filled[u.bank], 1)
                    elif kind == "stack":
                        j, g = at[1:]
                        if g == 0:
                            pe.wait_ge(qk_hi[l].sem, qk_hi[l].at(b, 2 * k + j + 1))
                            pe.wait_ge(qk_lo[l].sem, qk_lo[l].at(b, 2 * k + j + 1))
                        u = use["st", l, k, j, g]
                        open_bank(u)
                        out = bank(u.bank).bitcast(F16)
                        for h in range(8):
                            src = qks[l][:, j, k, g * 8 + h].rearrange("p s d -> p (s d)")
                            mm = te.transpose(out[0:QW, h * P:(h + 1) * P], src, identh)
                        mm.then_inc(filled[u.bank], 1)
                    elif kind == "maxima":
                        h = k
                        if h == 0:
                            all_read(pe, stacks(use, 1))
                        u = use["mx", 1, h]
                        open_bank(u)
                        for k in range(NT):
                            mm = te.matmul(bank(u.bank)[:, k * S:(k + 1) * S], qkT[1][0:QW, 0, h, k * P:(k + 1) * P],
                                           qkT[1][0:QW, 1, h, :], start=True, stop=True)
                        mm.then_inc(filled[u.bank], 1)
                    elif kind == "head":
                        head(l, b, k, use)
                    elif kind == "turn_out":
                        if k == 0:
                            all_read(pe, [use["o", l, g] for g in range(H // HG)])
                        turn(use["ot", l, k], xn[l][:, k, :], DC)
                    elif kind == "out_project":
                        if isinstance(i, int) and i == 0 and k == 0:
                            pe.wait_ge(w_split, len(W) // 2)
                            pe.wait_ge(consts_loaded, 16 * (len(row_names) + 1))
                        u = use["ot", l, k]
                        pe.wait_ge(read[u.bank], u.read_at)
                        u = use["y", l, k]
                        open_bank(u)
                        product(bank(u.bank), xT[l], wsplit[l, "o"], k, DC).then_inc(filled[u.bank], 1)
                    elif kind == "turn_ffn":
                        pe.wait_ge(xnF_ready.sem, xnF_ready.at(b, k + 1))
                        turn(use["xf", 0, k], xn[0][:, k, :], DC)
                    elif kind == "hadamard":
                        u = use["xf", 0, k]
                        pe.wait_ge(read[u.bank], u.read_at)
                        u = use["had", 0, k]
                        open_bank(u)
                        for c in range(DC):
                            for s in range(2):
                                mm = te.matmul(bank(u.bank), xT[0][:, s, c, k * P:(k + 1) * P], had_rows[c],
                                               start=(c + s == 0), stop=(c + s == DC))
                        mm.then_inc(filled[u.bank], 1)
                    elif kind == "turn_levels":
                        pe.wait_ge(nq_ready.sem, nq_ready.at(b, k + 1))
                        u = use["nt", 0, k]
                        open_bank(u)
                        for c in range(DC):
                            mm = te.transpose(bank(u.bank).bitcast(F16)[:, c * P:(c + 1) * P], nq[:, k, c * P:(c + 1) * P], identh)
                        mm.then_inc(filled[u.bank], 1)
                    elif kind == "ffn0":
                        if isinstance(i, int) and i == 0 and k == 0:
                            pe.wait_ge(setup_act, DC + 1)
                        u = use["nt", 0, k]
                        pe.wait_ge(read[u.bank], u.read_at)
                        u = use["f0", 0, k]
                        open_bank(u)
                        for c in range(DC):
                            mm = te.matmul(bank(u.bank), nT[:, c, k * P:(k + 1) * P], tern0[:, c, :],
                                           start=(c == 0), stop=(c == DC - 1))
                        mm.then_inc(filled[u.bank], 1)
                    tern, mean, signs = beside(i, (kind, l, *at), turn0_at, mean_first_at, turn_signs_at)
                    if tern is not None:
                        turn_tern0()
                    if mean is not None:
                        mean_all()
                    if signs is not None:
                        turn_signs(signs)
                if isinstance(i, int) and i == B + 1:
                    all_read(pe, [use["y", 1, k] for k in range(NT)])

            def stacks(use, l):
                return [use["st", l, k, j, g] for k in range(NT) for j in range(2) for g in range(2)]

            def head(l, b, n, use):
                if l == 1 and 1 <= n <= H:
                    h = n - 1
                    if h == 0:
                        pe.wait_ge(shift_ready.sem, shift_ready.at(b))
                    pe.wait_ge(clipped.sem, clipped.at(b, h + 1))
                    u = use["s", 1, h]
                    out = bank(u.bank).rearrange("p (k t n) -> p k t n", k=NT, t=NT)
                    for q in range(NT):
                        mm = te.matmul(out[:, :, q, :], mneg[:, q, h:h + 1].to_broadcast([P, P]),
                                       identh.unsqueeze(1).to_broadcast([P, NT, P]), start=False, stop=True,
                                       skip_group_check=True)
                    mm.then_inc(shifted.sem, 1)
                if n < H:
                    if n == 0 and l == 0:
                        all_read(pe, stacks(use, 0))
                    u = use["s", l, n]
                    open_bank(u)
                    for k in range(NT):
                        mm = te.matmul(bank(u.bank)[:, k * S:(k + 1) * S], qkT[l][0:QW, 1, n, k * P:(k + 1) * P],
                                       qkT[l][0:QW, 0, n, :], start=(k == 0), stop=True, skip_group_check=True)
                    mm.then_inc(filled[u.bank], 1)
                h = n - AV_LAG[l]
                if 0 <= h < H:
                    attend(l, b, h, use["o", l, h // HG])

            def attend(l, b, h, u):
                if h % HG == 0:
                    open_bank(u)
                if h == 0:
                    pe.wait_ge(v_lo[l].sem, v_lo[l].at(b))
                pe.wait_ge(p_lo[l].sem, p_lo[l].at(b, h + 1))
                for q in range(NT):
                    at = (q * HG + h % HG) * OW
                    out = bank(u.bank)[:, at:at + OW]
                    for k in range(NT):
                        p_hi_t = ph[l][:, h % NP, k * S + q * P:k * S + (q + 1) * P]
                        p_lo_t = pl[l][:, h % NP, k * S + q * P:k * S + (q + 1) * P]
                        te.matmul(out, p_hi_t, vs[l][:, k, h, 0:OW], start=(k == 0), stop=False)
                        te.matmul(out[:, 0:HD], p_hi_t, vs[l][:, k, h, HD + 2:VP], start=False, stop=False)
                        mm = te.matmul(out, p_lo_t, vs[l][:, k, h, 0:OW], start=False, stop=(k == NT - 1))
                mm.then_inc(av_done[l].sem, 1)

            steps(pe, step)

            def turn_b(s, k):
                pe.wait_ge(xnb_ready, s * BT + k + 1)
                later(pe, xTb_read, s * BT + k - 1)
                for c in range(DC):
                    mm = te.transpose(bank(6 + k % 2)[:, c * P:(c + 1) * P], xnb[:, k, c * P:(c + 1) * P], ident)
                mm.then_inc(xTb_filled, 1)

            def up(s, slot, f):
                later(pe, gelu_done, s * FC + f - 1)
                for c in range(DC):
                    for part in range(2):
                        mm = te.matmul(bank(4 + f % 2), w1T[:, c, f * P:(f + 1) * P], xTb[slot][:, part, c, :],
                                       start=(c + part == 0), stop=(c + part == DC))
                mm.then_inc(h_filled, 1)

            def down(s, f):
                g_lo_wait(pe, s, f)
                for k in range(BT):
                    if f == 0:
                        later(pe, yb_ready, s * BT - BT + k + 1)
                    for n, src in enumerate((gh, gl)):
                        mm = te.matmul(bank(k), src[:, f % NG, k * P:(k + 1) * P], w2T[:, f, :],
                                       start=(f + n == 0), stop=(f + n == FC))
                mm.then_inc(g_used, 1)

            def step_b(s, slot, r, has_next):
                for f in range(FC):
                    if has_next and 0 <= f - TURN_AT < BT:
                        turn_b(s + 1, f - TURN_AT)
                    down(s, f)
                    if f + 2 < FC:
                        up(s, slot, f + 2)
                    elif has_next:
                        if f + 2 == FC:
                            pe.wait_ge(xTb_read, s * BT + 2 * BT)
                        up(s + 1, 1 - slot, f + 2 - FC)

            pe.wait_ge(wtr_read, 4 * WC)
            for k in range(BT):
                turn_b(0, k)
            pe.wait_ge(xTb_read, BT)
            up(0, 0, 0)
            up(0, 0, 1)
            steps_b(step_b, pe)


_ROWS = ["L0_xattn_bq", "L0_xattn_bk", "L0_xattn_bv", "L0_xattn_bo", "L0_xattn_ln_gamma", "L0_xattn_ln_beta",
         "L1_xattn_bq", "L1_xattn_bk", "L1_xattn_bv", "L1_xattn_bo"]
_INS = ["x", "ctx_768", "L0_xattn_Wq", "L0_xattn_Wk", "L0_xattn_Wv", "L0_xattn_Wo", "L0_ffn_weight",
        "L1_xattn_Wq", "L1_xattn_Wk", "L1_xattn_Wv", "L1_xattn_Wo", "L1_ffn_W1", "L1_ffn_b1", "L1_ffn_W2",
        "L1_ffn_b2"] + _ROWS


def hadamard_signs():
    h = np.array([[1.0]])
    while h.shape[0] < P:
        h = np.block([[h, h], [h, -h]])
    return np.concatenate([h, -h, -h, h], axis=1).astype(np.float16)


def kernel(**inputs):
    from concourse import bacc
    from concourse.bass_utils import run_bass_kernel_spmd

    nc = bacc.Bacc("TRN2", target_bir_lowering=False, num_devices=1)
    arrays, t = {}, {}
    for name in _INS:
        arrays[f"in_{name}"] = np.ascontiguousarray(inputs[name])
    arrays["in_signs"] = hadamard_signs()
    for name, a in arrays.items():
        t[name[3:]] = nc.dram_tensor(name, a.shape, mybir.dt.from_np(a.dtype), kind="ExternalInput").ap()
    t["out"] = nc.dram_tensor("out_0", (B, S, D), F32, kind="ExternalOutput").ap()
    xattn_ffn(nc, t)
    r = run_bass_kernel_spmd(nc, [arrays], core_ids=[0])
    return r.results[0]["out_0"]
```
